# Optimizing a Trainium2 kernel written in Bass

```python
import numpy as np
import jax
import jax.numpy as jnp

def _softmax(x, axis=-1):
    return jax.nn.softmax(x, axis=axis)

def _gelu(x):
    return jax.nn.gelu(x, approximate=True)

def _silu(x):
    return jax.nn.silu(x)

def _sigmoid(x):
    return jax.nn.sigmoid(x)

def _layernorm(x, axis=-1, eps=1e-05):
    m = jnp.mean(x, axis=axis, keepdims=True)
    v = jnp.var(x, axis=axis, keepdims=True)
    return (x - m) / jnp.sqrt(v + eps)

def _scatter_add(tgt, idx, src, axis=0):
    return tgt.at[idx].add(src)

def _segment_sum(src, seg, n):
    return jax.ops.segment_sum(src, seg, n)
kernel_name = 'mk_flamingo_gated_d1_seqx_r2_4d47ee'

def setup_inputs(seed: int=0):
    np.random.seed(seed)
    _w = jnp.asarray

    def _rec_inputs():
        import jax
        import jax.numpy as jnp
        _rk = jax.random.key(seed)
        x = 7.22e-05 + 1 * jax.random.normal(jax.random.fold_in(_rk, 1), (32, 224, 512), jnp.float32)
        _lenS = 224 - jax.random.randint(jax.random.fold_in(_rk, 7), (32,), 0, max(1, 224 // 4) + 1, jnp.int32)
        _lenS2 = 750 - jax.random.randint(jax.random.fold_in(_rk, 8), (32,), 0, max(1, 750 // 4) + 1, jnp.int32)
        _ctx_1024P = jax.random.normal(jax.random.fold_in(_rk, 11), (32, 16, 512), jnp.float32)
        _ctx_1024c = jax.random.dirichlet(jax.random.fold_in(_rk, 511), 0.3 * jnp.ones((16,), jnp.float32), (32, 750))
        _ctx_1024t = jnp.einsum('bsk,bkd->bsd', _ctx_1024c, _ctx_1024P)
        _ctx_1024t = _ctx_1024t * jax.lax.rsqrt(jnp.mean(jnp.square(_ctx_1024t)) + 1e-12) * 0.953939
        ctx_1024 = 4.13588e-05 + 0.999923 * (_ctx_1024t + 0.3 * jax.random.normal(jax.random.fold_in(_rk, 611), (32, 750, 512), jnp.float32))
        _g = jax.random.normal(jax.random.fold_in(_rk, 9001), (2, 1), jnp.float32)
        _g = jnp.sign(_g) * jnp.maximum(jnp.abs(_g), 1.0) + (_g == 0) * 1.0
        g_xattn = _g[0]
        g_ffn = _g[1]
        return (x, ctx_1024, g_xattn, g_ffn)
    x, ctx_1024, g_xattn, g_ffn = _rec_inputs()

    def _L0_xattn_setup():
        import jax, jax.numpy as jnp
        import numpy as np
        C = 512
        B, SQ, SKV = (4, 1024, 1024)
        key = jax.random.key(seed)
        ks = jax.random.split(key, 10)
        s = 1.0 / np.sqrt(C)
        return {'x': jax.random.normal(ks[0], (B, SQ, C), jnp.float32), 'content_embeddings': jax.random.normal(ks[1], (B, SKV, C), jnp.float32), 'Wq': jax.random.normal(ks[2], (C, C), jnp.float32) * s, 'bq': jnp.zeros((C,), jnp.float32), 'Wk': jax.random.normal(ks[3], (C, C), jnp.float32) * s, 'bk': jnp.zeros((C,), jnp.float32), 'Wv': jax.random.normal(ks[4], (C, C), jnp.float32) * s, 'bv': jnp.zeros((C,), jnp.float32), 'Wo': jax.random.normal(ks[5], (C, C), jnp.float32) * s, 'bo': jnp.zeros((C,), jnp.float32)}
    _L0_xattn_all = _L0_xattn_setup()
    _L0_xattn_in = {k: v for k, v in _L0_xattn_all.items() if k in ('Wq', 'bq', 'Wk', 'bk', 'Wv', 'bv', 'Wo', 'bo')}
    del _L0_xattn_all

    def _L0_ffn_setup():
        import jax, jax.numpy as jnp
        import numpy as np
        DM, NEXPERTS, SETS, ESIZE = (512, 32, 4, 32)
        B, S = (2, 4096)
        key = jax.random.key(seed)
        ks = jax.random.split(key, 7)
        sc = 0.02
        return {'x': jax.random.normal(ks[0], (B, S, DM), jnp.float32), 'Wc': jax.random.normal(ks[1], (DM, NEXPERTS, SETS), jnp.float32) * sc, 'bc': jax.random.normal(ks[2], (NEXPERTS, SETS), jnp.float32) * sc, 'W1': jax.random.normal(ks[3], (NEXPERTS, SETS, DM, ESIZE), jnp.float32) * sc, 'b1': jax.random.normal(ks[4], (NEXPERTS, SETS, ESIZE), jnp.float32) * sc, 'W2': jax.random.normal(ks[5], (NEXPERTS, SETS, DM, ESIZE), jnp.float32) * sc, 'b2': jax.random.normal(ks[6], (NEXPERTS, SETS, DM), jnp.float32) * sc}
    _L0_ffn_all = _L0_ffn_setup()
    _L0_ffn_in = {k: v for k, v in _L0_ffn_all.items() if k in ('Wc', 'bc', 'W1', 'b1', 'W2', 'b2')}
    del _L0_ffn_all
    return {'x': x, 'ctx_1024': ctx_1024, 'g_xattn': g_xattn, 'g_ffn': g_ffn, 'L0_xattn_Wq': _L0_xattn_in['Wq'], 'L0_xattn_bq': _L0_xattn_in['bq'], 'L0_xattn_Wk': _L0_xattn_in['Wk'], 'L0_xattn_bk': _L0_xattn_in['bk'], 'L0_xattn_Wv': _L0_xattn_in['Wv'], 'L0_xattn_bv': _L0_xattn_in['bv'], 'L0_xattn_Wo': _L0_xattn_in['Wo'], 'L0_xattn_bo': _L0_xattn_in['bo'], 'L0_ffn_Wc': _L0_ffn_in['Wc'], 'L0_ffn_bc': _L0_ffn_in['bc'], 'L0_ffn_W1': _L0_ffn_in['W1'], 'L0_ffn_b1': _L0_ffn_in['b1'], 'L0_ffn_W2': _L0_ffn_in['W2'], 'L0_ffn_b2': _L0_ffn_in['b2']}

def reference(x, ctx_1024, g_xattn, g_ffn, L0_xattn_Wq, L0_xattn_bq, L0_xattn_Wk, L0_xattn_bk, L0_xattn_Wv, L0_xattn_bv, L0_xattn_Wo, L0_xattn_bo, L0_ffn_Wc, L0_ffn_bc, L0_ffn_W1, L0_ffn_b1, L0_ffn_W2, L0_ffn_b2):
    import jax
    import jax.numpy as jnp

    def _L0_xattn_ref(x, content_embeddings, Wq, bq, Wk, bk, Wv, bv, Wo, bo):
        import jax, jax.numpy as jnp
        import numpy as np
        C = 512
        B, SQ, SKV = (4, 1024, 1024)
        queries = x @ Wq.T + bq
        keys = content_embeddings @ Wk.T + bk
        values = content_embeddings @ Wv.T + bv
        scale = 1.0 / jnp.sqrt(jnp.asarray(C, x.dtype))
        scores = jnp.einsum('bqc,bkc->bqk', queries, keys) * scale
        attn = jax.nn.softmax(scores, axis=-1)
        attended = jnp.einsum('bqk,bkc->bqc', attn, values)
        out = x + attended
        return out @ Wo.T + bo

    def _L0_ffn_ref(x, Wc, bc, W1, b1, W2, b2):
        import jax, jax.numpy as jnp
        import numpy as np
        DM, NEXPERTS, SETS, ESIZE = (512, 32, 4, 32)
        B, S = (2, 4096)
        b, s, d = x.shape
        g = Wc.shape[1]
        grouped = x.reshape(b, s // g, g, d)
        logits = jnp.einsum('bntd,des->bntes', grouped, Wc) + bc
        tie = jnp.linspace(0.0, 1e-06, g, dtype=x.dtype).reshape(-1, 1, 1)
        logits = logits + tie
        perm = (logits == jnp.max(logits, axis=-3, keepdims=True)).astype(x.dtype)
        permuted = jnp.einsum('bntd,bntes->bnesd', grouped, perm)
        inner = jax.nn.relu(jnp.einsum('bnesd,esdf->bnesf', permuted, W1) + b1)
        result_permuted = jnp.einsum('bnesf,esdf->bnesd', inner, W2) + b2
        result = jnp.einsum('bnesd,bntes->bntd', result_permuted, perm)
        return result.reshape(b, s, d)
    x = x + jnp.tanh(g_xattn[0]) * _L0_xattn_ref(_layernorm(x, axis=-1), ctx_1024, L0_xattn_Wq, L0_xattn_bq, L0_xattn_Wk, L0_xattn_bk, L0_xattn_Wv, L0_xattn_bv, L0_xattn_Wo, L0_xattn_bo)
    x = x + jnp.tanh(g_ffn[0]) * _L0_ffn_ref(_layernorm(x, axis=-1), L0_ffn_Wc, L0_ffn_bc, L0_ffn_W1, L0_ffn_b1, L0_ffn_W2, L0_ffn_b2)
    return x

_drawn_inputs = setup_inputs


def setup_inputs(seed=0):
    import zlib

    import numpy as np

    out = dict(_drawn_inputs(seed))
    spreads = {'L0_xattn_bq': (0.0, 0.588),
     'L0_xattn_bk': (0.0, 2.0),
     'L0_xattn_bv': (0.0, 0.1),
     'L0_xattn_bo': (0.0, 0.1)}
    factors = {'L0_ffn_b1': 26.184}
    for name, (base, spread) in spreads.items():
        noise = np.random.default_rng([zlib.crc32(name.encode()), seed]).standard_normal(out[name].shape)
        drawn = base * np.exp(spread * noise) if base else spread * noise
        out[name] = jnp.asarray(drawn.astype(out[name].dtype))
    for name, factor in factors.items():
        out[name] = (out[name] * factor).astype(out[name].dtype)
    return out
```

```python
import concourse.bass as bass
from concourse import mybir
from contextlib import ExitStack
import numpy as np

F32 = mybir.dt.float32
F32R = mybir.dt.float32r
F16 = mybir.dt.float16
ALU = mybir.AluOpType
ACT = mybir.ActivationFunctionType
AX = mybir.AxisListType

P = 128
BANK = 512
EPS = 1e-5
UP = 256.0
TIE = 1e-6


def ev(index, per, k=0):
    return per * index + k + 1


class Shapes:

    def __init__(self, x, ctx, wc, w1):
        self.B, self.Q, self.C = x.shape
        self.K = ctx.shape[1]
        self.G, self.S = wc.shape[1:]
        self.ES = self.G * self.S
        self.F = w1.shape[3]
        self.DT = self.C // P
        self.QT = [(0, P), (P, self.Q - P)]
        self.KP = 125
        self.KC = self.K // self.KP
        self.NB = self.Q // self.G
        self.T = self.B * self.Q
        self.N = self.T // self.G


def wait_apart(eng, sem, value, passed):
    eng.wait_ge(sem, value)
    eng.sem_inc(passed, 1)


def attention_and_routing(nc, sh, a, scratch, permT_all):
    B, Q, C, K, DT, KP, KC, QT = sh.B, sh.Q, sh.C, sh.K, sh.DT, sh.KP, sh.KC, sh.QT
    G, NB, ES = sh.G, sh.NB, sh.ES
    SCALE = float(C) ** -0.5
    KH = K // 2
    KW = KH + KH % 2
    x_d, ctx_d = a["x"], a["ctx_1024"]
    ctx_v = ctx_d.rearrange("b (p c) d -> b p c d", c=KC)

    with ExitStack() as es:
        def sb(name, shape, dt=F32):
            return es.enter_context(nc.sbuf_tensor(name, shape, dt))

        def sem(name):
            return es.enter_context(nc.semaphore(name))

        qkH, qkL = (sb(f"w_qk{h}", [P, DT, C], F32R) for h in "HL")
        woH, woL = (sb(f"w_o{h}", [P, DT, C], F32R) for h in "HL")
        wvoH, wvoL = (sb(f"w_vo{h}", [P, DT, C], F32R) for h in "HL")
        qk_bias = sb("qk_bias", [P, DT])
        key_bias_row = sb("key_bias_row", [P, C])
        key_bias_const = sb("key_bias_const", [P, 1])
        out_bias_row = sb("out_bias_row", [P, C])
        gate = sb("gate", [P, 1])
        wc = sb("wc", [P, DT, ES])
        bc = sb("bc", [P, 1])
        tie = sb("tie", [P, NB, G])
        ident = sb("ident", [P, P])
        minus_half = sb("minus_half", [P, 2])
        mv1, mv2 = (sb(f"mean_var{n}", [P, 2, 2]) for n in (1, 2))

        def weights():
            with ExitStack() as ws:
                def wb(name, shape, dt=F32):
                    return ws.enter_context(nc.sbuf_tensor(name, shape, dt))

                def wsem(name):
                    return ws.enter_context(nc.semaphore(name))

                raw = {n: wb(f"raw_{n}", [P, DT, C]) for n in ("Wq", "Wk", "Wv", "Wo")}
                cols = wb("bias_cols", [P, 3, DT])
                wide = wb("bias_wide", [P, 2, DT, P])
                woT = wb("woT", [P, DT, C])
                bo_row = wb("bo_row", [P, C])
                g_raw = wb("g_raw", [P, 1])
                ps = ws.enter_context(nc.psum_tensor("ps_weights", [P, 8, BANK], F32))
                loaded = {n: wsem(f"{n}_loaded") for n in raw}
                small = wsem("small_loaded")
                iota = wsem("constants_made")
                wide_made = wsem("wide_made")
                turned = wsem("wo_turned")
                turned_copied = wsem("wo_turned_copied")
                product = wsem("product_ready")
                high = wsem("high_half_made")
                low = wsem("low_half_made")
                rows = wsem("row_ready")
                rows_out = wsem("row_copied")
                gate_done = wsem("gate_done")
                summed = wsem("bias_summed")

                with nc.Block() as block:
                    @block.sync
                    def _(sp):
                        for n in ("Wo", "Wq", "Wk", "Wv"):
                            sp.dma_start(raw[n][:, :, :], a[f"L0_xattn_{n}"].rearrange("(t p) c -> p t c", p=P)).then_inc(loaded[n], 16)
                        for n, name in enumerate(("bq", "bk", "bv")):
                            with nc.allow_non_contiguous_dma(reason="a bias as columns"):
                                sp.dma_start(cols[:, n, :], a[f"L0_xattn_{name}"].rearrange("(t p) -> p t", p=P)).then_inc(small, 16)
                        sp.dma_start(bo_row[:, :], a["L0_xattn_bo"].rearrange("(o c) -> o c", o=1).broadcast_to([P, C])).then_inc(small, 16)
                        sp.dma_start(g_raw[:, :], a["g_xattn"].rearrange("(o c) -> o c", o=1).broadcast_to([P, 1])).then_inc(small, 16)
                        sp.dma_start(wc[:, :, :], a["L0_ffn_Wc"].rearrange("(t p) e s -> p t (e s)", p=P)).then_inc(small, 16)
                        with nc.allow_non_contiguous_dma(reason="a bias as a column"):
                            sp.dma_start(bc[:, :], a["L0_ffn_bc"].rearrange("e (s o) -> (e s) o", o=1)).then_inc(small, 16)

                    @block.gpsimd
                    def _(pool):
                        pool.memset(ident[:, :], 0.0).then_inc(iota, 1)
                        pool.memset(minus_half[:, :], -0.5).then_inc(iota, 1)
                        pool.wait_ge(iota, 2)
                        pool.affine_select(out=ident[:, :], in_=ident[:, :], compare_op=ALU.not_equal, fill=1.0,
                                           base=0, pattern=[[-1, P]], channel_multiplier=1).then_inc(iota, 1)
                        for mv in (mv1, mv2):
                            pool.memset(mv[:, :, :], 0.0).then_inc(iota, 1)
                        ties = np.linspace(0.0, TIE, G, dtype=np.float32)
                        for t in range(G):
                            pool.memset(tie[:, :, t], float(ties[t])).then_inc(iota, 1)

                    @block.tensor
                    def _(pe):
                        pe.wait_ge(iota, 3)
                        pe.wait_ge(loaded["Wo"], 16)
                        for t in range(DT):
                            for o in range(DT):
                                mm = pe.transpose(ps[:, t, o * P:(o + 1) * P], raw["Wo"][:, o, t * P:(t + 1) * P], ident[:, :])
                            mm.then_inc(turned, 1)
                        pe.wait_ge(loaded["Wq"], 16)
                        pe.wait_ge(loaded["Wk"], 16)
                        for t in range(DT):
                            for h in range(DT):
                                mm = pe.matmul(ps[:, 4 + t, :], raw["Wq"][:, h, t * P:(t + 1) * P], raw["Wk"][:, h, :],
                                               start=(h == 0), stop=(h == DT - 1))
                            mm.then_inc(product, 1)
                        pe.wait_ge(loaded["Wv"], 16)
                        pe.wait_ge(turned_copied, DT)
                        pe.wait_ge(low, DT)
                        for t in range(DT):
                            for h in range(DT):
                                mm = pe.matmul(ps[:, t, :], raw["Wv"][:, h, t * P:(t + 1) * P], woT[:, h, :],
                                               start=(h == 0), stop=(h == DT - 1))
                            mm.then_inc(product, 1)
                        pe.wait_ge(wide_made, 2)
                        pe.wait_ge(low, 2 * DT)
                        for h in range(DT):
                            mm = pe.matmul(ps[:, 4, :], wide[:, 0, h, :], woT[:, h, :], start=(h == 0), stop=(h == DT - 1))
                        mm.then_inc(rows, 1)
                        for h in range(DT):
                            mm = pe.matmul(ps[:, 5, :], wide[:, 1, h, :], raw["Wq"][:, h, :], start=(h == 0), stop=(h == DT - 1))
                        mm.then_inc(rows, 1)
                        for t in range(DT):
                            for h in range(DT):
                                mm = pe.matmul(ps[:, 6, t:t + 1], raw["Wk"][:, h, t * P:(t + 1) * P], cols[:, 0, h:h + 1],
                                               start=(h == 0), stop=(h == DT - 1))
                        mm.then_inc(rows, 1)
                        for h in range(DT):
                            mm = pe.matmul(ps[:, 7, 0:1], wide[:, 1, h, :], cols[:, 0, h:h + 1], start=(h == 0), stop=(h == DT - 1))
                        mm.then_inc(rows, 1)

                    @block.scalar
                    def _(act):
                        act.wait_ge(small, 16 * 7)
                        act.activation(gate[:, :], g_raw[:, :], ACT.Tanh).then_inc(gate_done, 1)
                        for t in range(DT):
                            act.wait_ge(turned, t + 1)
                            act.activation(woH[:, t, :], ps[:, t, :], ACT.Copy).then_inc(high, 1)
                        for n in range(2 * DT):
                            act.wait_ge(product, n + 1)
                            dst, bank = (qkH, 4 + n) if n < DT else (wvoH, n - DT)
                            act.activation(dst[:, n % DT, :], ps[:, bank, :], ACT.Copy).then_inc(high, 1)

                    @block.vector
                    def _(dve):
                        dve.wait_ge(small, 16 * 7)
                        for n, col in enumerate((2, 1)):
                            dve.tensor_copy(wide[:, n, :, :], cols[:, col, :].unsqueeze(2).broadcast_to([P, DT, P])).then_inc(wide_made, 1)
                        for t in range(DT):
                            dve.wait_ge(high, t + 1)
                            dve.tensor_copy(woT[:, t, :], ps[:, t, :]).then_inc(turned_copied, 1)
                            dve.wait_ge(turned_copied, t + 1)
                            dve.tensor_tensor(woL[:, t, :], woT[:, t, :], woH[:, t, :].bitcast(F32), ALU.subtract).then_inc(low, 1)
                        for n in range(2 * DT):
                            dve.wait_ge(high, DT + n + 1)
                            hi, lo, bank = (qkH, qkL, 4 + n) if n < DT else (wvoH, wvoL, n - DT)
                            dve.tensor_tensor(lo[:, n % DT, :], ps[:, bank, :], hi[:, n % DT, :].bitcast(F32), ALU.subtract).then_inc(low, 1)
                        dve.wait_ge(rows, 4)
                        dve.tensor_tensor(out_bias_row[:, :], ps[:, 4, :], bo_row[:, :], ALU.add).then_inc(summed, 1)
                        dve.wait_ge(summed, 1)
                        dve.wait_ge(gate_done, 1)
                        dve.tensor_scalar(out_bias_row[:, :], out_bias_row[:, :], gate[:, :], None, ALU.mult).then_inc(rows_out, 1)
                        dve.tensor_copy(key_bias_row[:, :], ps[:, 5, :]).then_inc(rows_out, 1)
                        dve.tensor_copy(qk_bias[:, :], ps[:, 6, 0:DT]).then_inc(rows_out, 1)
                        dve.tensor_copy(key_bias_const[:, :], ps[:, 7, 0:1]).then_inc(rows_out, 1)

        weights()

        ctx_raw = [sb(f"ctx_raw{p}", [KP, KC, C]) for p in range(2)]
        ctxH, ctxL = (sb(f"ctx{h}", [KP, KC, C], F32R) for h in "HL")
        ctxTH, ctxTL = (sb(f"ctxT{h}", [P, DT, K], F32R) for h in "HL")
        x = [sb(f"x{p}", [P, 2, C]) for p in range(2)]
        xn = sb("xn", [P, 2, C])
        xnTH, xnTL = (sb(f"xnT{h}", [P, DT, Q], F32R) for h in "HL")
        atH, atL = (sb(f"at{h}", [P, DT, Q], F32R) for h in "HL")
        probs = sb("probs", [P, 2, K])
        pTH, pTL = (sb(f"probsT{h}", [KP, KC, Q], F32R) for h in "HL")
        oTH, oTL = (sb(f"oT{h}", [P, DT, Q], F32R) for h in "HL")
        xn2 = sb("xn2", [P, 2, C])
        dot_junk = sb("dot_junk", [P, C], F16)
        halves = sb("token_halves", [P, 2, 2, C], F16)
        xn2T = sb("xn2T", [P, DT, Q])
        logits = sb("logits", [P, 2, NB, G])
        st1, st2 = (sb(f"bn_stats{n}", [P, 2, 6]) for n in (1, 2))
        ve1, ve2 = (sb(f"var_eps{n}", [P, 2]) for n in (1, 2))
        rs1, rs2 = (sb(f"rstd{n}", [P, 2]) for n in (1, 2))
        kb = sb("query_key_bias", [P, 2, 2])
        top = sb("row_max", [P, 2])
        shift = sb("exp_shift", [P, 2, 2])
        total = sb("prob_sum", [P, 2])
        share = sb("gate_over_sum", [P, 2, 2])
        best = sb("best_logit", [P, NB])
        ps = es.enter_context(nc.psum_tensor("ps", [P, 8 * BANK], F32))

        ctx_in = [sem(f"ctx_in{p}") for p in range(2)]
        x_in = [sem(f"x_in{p}") for p in range(2)]
        x_out = [sem(f"x_out{p}") for p in range(2)]
        xn_in = sem("xn_in")
        halves_out = sem("halves_out")
        ctxT_ready, ctxT_high, ctxT_low = sem("ctxT_ready"), sem("ctxT_high"), sem("ctxT_low")
        xnT_ready, xnT_high, xnT_low = sem("xnT_ready"), sem("xnT_high"), sem("xnT_low")
        at_ready, at_high, at_low = sem("at_ready"), sem("at_high"), sem("at_low")
        scores_ready, probs_ready = sem("scores_ready"), sem("probs_ready")
        pT_ready, pT_high, pT_low = sem("pT_ready"), sem("pT_high"), sem("pT_low")
        oT_ready, oT_high, oT_low = sem("oT_ready"), sem("oT_high"), sem("oT_low")
        direct_ready, direct_added = sem("direct_ready"), sem("direct_added")
        attended_ready, attended_added = sem("attended_ready"), sem("attended_added")
        xn2T_ready, xn2T_copied = sem("xn2T_ready"), sem("xn2T_copied")
        logits_ready, logits_read = sem("logits_ready"), sem("logits_read")
        ctx_high, ctx_low = sem("ctx_high"), sem("ctx_low")
        stats1, meanvar1, vareps1, rstd1, xn_ready = (sem(n) for n in ("stats1", "meanvar1", "vareps1", "rstd1", "xn_ready"))
        stats2, meanvar2, vareps2, rstd2, xn2_ready = (sem(n) for n in ("stats2", "meanvar2", "vareps2", "rstd2", "xn2_ready"))
        keydot, keybias = sem("keydot"), sem("keybias")
        bias_added = sem("bias_added")
        passed_dve, passed_pool = sem("passed_by_dve"), sem("passed_by_pool")
        rowmax, shift_part, shift_ready = sem("rowmax"), sem("shift_part"), sem("shift_ready")
        recip, share_ready = sem("recip"), sem("share_ready")
        half_high, half_low = sem("half_high"), sem("half_low")
        best_found, perm_ready = sem("best_found"), sem("perm_ready")

        def parts(v):
            return v.rearrange("n (t p) -> n t p", t=DT)

        def by_part(v):
            return v.rearrange("n (p t) -> n t p", t=DT)

        def bank(n, rows=P, cols=BANK):
            return ps[0:rows, n * BANK:n * BANK + cols]

        FILLS = ([("xnT", n, 1) for n in range(2)] + [("xn2T", n, -1) for n in range(2)] + [("pT", n, 0) for n in range(3)]
                 + [("ctxT", 0, 1), ("logits", 0, -1)] + [("ctxT", n, 1) for n in range(1, 8)])
        FREED = {"xn2T": (xn2T_copied, 2), "ctxT": (ctxT_low, 8), "logits": (logits_read, 1), "pT": (pT_low, 3), "xnT": (xnT_low, 2)}

        def ring(kind, n):
            at = next(f for f, (k, m, _) in enumerate(FILLS) if (k, m) == (kind, n))
            return at, 4 + at % 4

        def exists(step, batch_off):
            if not isinstance(step, int):
                return True
            return 0 <= step + batch_off < B

        def wait_ring(pe, step, kind, n):
            at, _ = ring(kind, n)
            back = 0
            while True:
                at -= 4
                if at < 0:
                    at, back = at + len(FILLS), back + 1
                k, m, off = FILLS[at]
                if isinstance(step, int) and step - back < -1:
                    return
                if not isinstance(step, int) or exists(step - back, off):
                    freed, per = FREED[k]
                    pe.wait_ge(freed, ev(step - back + off, per, m))
                    return

        def steps(eng, one):
            one(-2, 0)
            one(-1, 1)
            one(0, 0)
            if B > 2:
                one(1, 1)
            pairs = max((B - 4) // 2, 0)
            if pairs:
                with eng.Fori(1, 1 + pairs) as m:
                    one(2 * m, 0)
                    one(2 * m + 1, 1)
            for s in range(2 + 2 * pairs, B - 1):
                one(s, s % 2)
            one(B - 1, (B - 1) % 2)
            one(B, B % 2)

        def flags(s):
            if not isinstance(s, int):
                return True, True, True, True
            return s >= 1, 0 <= s < B, 0 <= s + 1 < B, s + 2 < B

        def ctx_arrived(b, par):
            return 8 * (b - par) + 16

        def x_arrived(b, par):
            return 16 * (b - par) + 32

        def score_view(q):
            n = QT[q][1]
            at = 2 * q * BANK
            skip = BANK + KW - KH
            return ps[0:n, at:at + 2 * skip].rearrange("p (a b) -> p a b", b=skip)[:, :, 0:KH]

        with nc.Block() as block:
            @block.sync
            def _(sp):
                def load_x(b, par):
                    for q, (q0, n) in enumerate(QT):
                        sp.dma_start(x[par][0:n, q, :], x_d[b, q0:q0 + n, :]).then_inc(x_in[par], 16)

                def one(s, par):
                    tail, now, nxt, after = flags(s)
                    if isinstance(s, int) and s < 0 and nxt:
                        load_x(0, 0)
                        sp.dma_start(ctx_raw[1][:, :, :], ctx_v[1]).then_inc(ctx_in[1], 16)
                        load_x(1, 1)
                    if tail:
                        t = s - 1
                        o = 1 - par
                        for q, (q0, n) in enumerate(QT):
                            sp.wait_ge(attended_added, ev(t, 2, q))
                            sp.dma_start(scratch["x2"][t, q0:q0 + n, :], x[o][0:n, q, :]).then_inc(x_out[o], 16)
                    if now and after:
                        sp.wait_ge(ctxT_ready, ev(s, 8, 7))
                        sp.wait_ge(ctx_low, ev(s, KC, KC - 1))
                        sp.dma_start(ctx_raw[par][:, :, :], ctx_v[s + 2]).then_inc(ctx_in[par], 16)
                    if tail and nxt:
                        sp.wait_ge(x_out[o], 16 * (t - o) + 32)
                        sp.wait_ge(xn2_ready, ev(t, 2, 1))
                        load_x(s + 1, o)
                    if tail:
                        for q, (q0, n) in enumerate(QT):
                            sp.wait_ge(half_low, ev(t, 2, q))
                            sp.dma_start(scratch["halves"][t, q0:q0 + n, :, :], halves[0:n, q, :, :]).then_inc(halves_out, 16)
                    if after:
                        if nxt:
                            sp.wait_ge(xnT_ready, ev(s + 1, 2, 1))
                            sp.wait_ge(keydot, ev(s + 1, 2, 1))
                        for q, (q0, n) in enumerate(QT):
                            sp.dma_start(xn[0:n, q, :], x_d[s + 2, q0:q0 + n, :]).then_inc(xn_in, 16)
                        if not nxt:
                            sp.dma_start(ctx_raw[0][:, :, :], ctx_v[0]).then_inc(ctx_in[0], 16)
                    if isinstance(s, int) and s == B:
                        for o in range(2):
                            sp.wait_ge(x_out[o], 32 * (B // 2 if B % 2 == 0 else (B + 1 - o) // 2))
                        sp.wait_ge(halves_out, 32 * B)

                steps(sp, one)

            @block.gpsimd
            def _(pool):
                def one(s, par):
                    tail, now, nxt, after = flags(s)

                    def rstd(b, meanvar, mv, ve, vareps, rs, rs_sem):
                        wait_apart(pool, meanvar, ev(b, 2, 1), passed_pool)
                        pool.tensor_scalar(ve[:, :], mv[:, :, 1], EPS, 1.0, ALU.add, ALU.mult).then_inc(vareps, 1)
                        wait_apart(pool, vareps, ev(b, 1), passed_pool)
                        pool.tensor_tensor(rs[:, :], ve[:, :], minus_half[:, 0:2], ALU.pow).then_inc(rs_sem, 1)

                    if tail:
                        rstd(s - 1, meanvar2, mv2, ve2, vareps2, rs2, rstd2)
                    if nxt:
                        pool.wait_ge(x_in[1 - par], x_arrived(s + 1, 1 - par))
                        for q, (_, n) in enumerate(QT):
                            xv = x[1 - par][0:n, q, :]
                            pool.tensor_tensor(xv, xv, out_bias_row[0:n, :], ALU.add).then_inc(bias_added, 1)
                    if after:
                        rstd(s + 2, meanvar1, mv1, ve1, vareps1, rs1, rstd1)
                    if nxt:
                        for c in range(KC):
                            pool.wait_ge(ctx_high, ev(s + 1, KC, c))
                            pool.tensor_tensor(ctxL[:, c, :], ctx_raw[1 - par][:, c, :], ctxH[:, c, :].bitcast(F32),
                                               ALU.subtract).then_inc(ctx_low, 1)

                steps(pool, one)

            @block.scalar
            def _(act):
                def one(s, par):
                    tail, now, nxt, _ = flags(s)
                    t, f = s - 1, s + 1

                    def exps(q):
                        n = QT[q][1]
                        act.wait_ge(shift_ready, ev(s, 2, q))
                        if not isinstance(s, int) or s >= 1:
                            act.wait_ge(pT_ready, ev(s - 1, 3, 2))
                        act.activation(probs[0:n, q, :].rearrange("p (a b) -> p a b", b=KH), score_view(q),
                                       ACT.Exp, bias=shift[0:n, q, 1:2], scale=SCALE,
                                       accum_out=total[0:n, q:q + 1]).then_inc(probs_ready, 1)

                    def high_pair(dst, kind, b, per, n, ready, done, rows=P):
                        act.wait_ge(ready, ev(b, per, n))
                        _, bk = ring(kind, n)
                        act.activation(dst[:, 2 * n:2 * n + 2, :], bank(bk, rows, 2 * Q).rearrange("p (a q) -> p a q", a=2),
                                       ACT.Copy).then_inc(done, 1)

                    def at_highs(h):
                        act.wait_ge(at_ready, ev(f, 2, h))
                        for m in (2 * h, 2 * h + 1):
                            act.activation(atH[:, m, :], bank(h)[:, m % 2 * Q:m % 2 * Q + Q], ACT.Identity,
                                           bias=qk_bias[:, m:m + 1]).then_inc(at_high, 1)

                    def ctxT_highs(ns):
                        for n in ns:
                            act.wait_ge(ctxT_ready, ev(f, 8, n))
                            _, bk = ring("ctxT", n)
                            act.activation(ctxTH[:, n // 2, n % 2 * KH:n % 2 * KH + KH], bank(bk, P, KH), ACT.Copy).then_inc(ctxT_high, 1)

                    def oT_highs(h):
                        act.wait_ge(oT_ready, ev(s, 2, h))
                        act.activation(oTH[:, 2 * h:2 * h + 2, :], bank(2 + h, P, 2 * Q).rearrange("p (a q) -> p a q", a=2),
                                       ACT.Copy).then_inc(oT_high, 1)

                    if now:
                        exps(0)
                    if nxt:
                        if now:
                            act.wait_ge(direct_ready, ev(f - 1, 2, 1))
                        for h in range(2):
                            high_pair(xnTH, "xnT", f, 2, h, xnT_ready, xnT_high)
                    if tail:
                        if not isinstance(s, int) or t >= 1:
                            act.wait_ge(halves_out, 32 * t)
                        for q, (_, n) in enumerate(QT):
                            act.wait_ge(xn2_ready, ev(t, 2, q))
                            act.activation(parts(halves[0:n, q, 0, :]), by_part(xn2[0:n, q, :]), ACT.Copy, scale=UP).then_inc(half_high, 1)
                    if now:
                        exps(1)
                    if nxt:
                        at_highs(0)
                    if tail:
                        for h in range(2):
                            high_pair(xn2T, "xn2T", t, 2, h, xn2T_ready, xn2T_copied)
                    if nxt:
                        at_highs(1)
                    if now:
                        if not isinstance(s, int) or s >= 1:
                            act.wait_ge(oT_ready, ev(s - 1, 2, 1))
                        for n in range(3):
                            high_pair(pTH, "pT", s, 3, n, pT_ready, pT_high, KP)
                    if nxt:
                        if now:
                            act.wait_ge(scores_ready, ev(s, 2, 1))
                        ctxT_highs(range(4))
                    if now:
                        if not isinstance(s, int) or s >= 1:
                            act.wait_ge(attended_ready, ev(s - 1, 2, 1))
                        oT_highs(0)
                    if nxt:
                        ctxT_highs(range(4, 8))
                    if now:
                        oT_highs(1)
                    if nxt:
                        act.wait_ge(ctx_in[1 - par], ctx_arrived(f, 1 - par))
                        for c in range(KC):
                            act.activation(ctxH[:, c, :], ctx_raw[1 - par][:, c, :], ACT.Copy).then_inc(ctx_high, 1)

                steps(act, one)

            @block.vector
            def _(dve):
                def one(s, par):
                    tail, now, nxt, after = flags(s)
                    t, f, g = s - 1, s + 1, s + 2
                    xt = xf = x[1 - par]
                    if tail:
                        for q, (_, n) in enumerate(QT):
                            dve.wait_ge(attended_ready, ev(t, 2, q))
                            dve.wait_ge(direct_added, ev(t, 2, q))
                            dve.wait_ge(share_ready, ev(t, 2, q))
                            dve.scalar_tensor_tensor(xt[0:n, q, :], bank(2 + q, n), share[0:n, q, 1:2], xt[0:n, q, :],
                                                     ALU.mult, ALU.add).then_inc(attended_added, 1)
                            dve.wait_ge(attended_added, ev(t, 2, q))
                            dve.bn_stats(st2[0:n, q, :], xt[0:n, q, :]).then_inc(stats2, 1)
                        for q, (_, n) in enumerate(QT):
                            wait_apart(dve, stats2, ev(t, 2, q), passed_dve)
                            dve.bn_aggr(mv2[0:n, q, :], st2[0:n, q, :]).then_inc(meanvar2, 1)

                    def maxes(q):
                        n = QT[q][1]
                        dve.wait_ge(scores_ready, ev(s, 2, q))
                        dve.tensor_reduce(top[0:n, q:q + 1], score_view(q), AX.XY, ALU.max).then_inc(rowmax, 1)
                        dve.wait_ge(rowmax, ev(s, 2, q))
                        dve.wait_ge(keybias, ev(s, 2, q))
                        dve.tensor_scalar(shift[0:n, q, 0:1], top[0:n, q:q + 1], kb[0:n, q, 1:2], -SCALE, ALU.add, ALU.mult).then_inc(shift_part, 1)
                        dve.wait_ge(shift_part, ev(s, 2, q))
                        dve.scalar_tensor_tensor(shift[0:n, q, 1:2], kb[0:n, q, 1:2], SCALE, shift[0:n, q, 0:1],
                                                 ALU.mult, ALU.add).then_inc(shift_ready, 1)

                    def low_pair(lo, hi, kind, b, per, n, high, done, rows=P):
                        dve.wait_ge(high, ev(b, per, n))
                        _, bk = ring(kind, n)
                        at = slice(2 * n, 2 * n + 2)
                        dve.tensor_tensor(lo[:, at, :], bank(bk, rows, 2 * Q).rearrange("p (a q) -> p a q", a=2),
                                          hi[:, at, :].bitcast(F32), ALU.subtract).then_inc(done, 1)

                    def at_lows(h):
                        dve.wait_ge(at_high, ev(f, 4, 2 * h + 1))
                        for m in (2 * h, 2 * h + 1):
                            ins = dve.scalar_tensor_tensor(atL[:, m, :], bank(h)[:, m % 2 * Q:m % 2 * Q + Q], qk_bias[:, m:m + 1],
                                                           atH[:, m, :].bitcast(F32), ALU.add, ALU.subtract)
                        ins.then_inc(at_low, 1)

                    def ctxT_lows(ns):
                        for n in ns:
                            dve.wait_ge(ctxT_high, ev(f, 8, n))
                            _, bk = ring("ctxT", n)
                            at = slice(n % 2 * KH, n % 2 * KH + KH)
                            dve.tensor_tensor(ctxTL[:, n // 2, at], bank(bk, P, KH), ctxTH[:, n // 2, at].bitcast(F32),
                                              ALU.subtract).then_inc(ctxT_low, 1)

                    def oT_lows(h):
                        dve.wait_ge(oT_high, ev(s, 2, h))
                        at = slice(2 * h, 2 * h + 2)
                        dve.tensor_tensor(oTL[:, at, :], bank(2 + h, P, 2 * Q).rearrange("p (a q) -> p a q", a=2),
                                          oTH[:, at, :].bitcast(F32), ALU.subtract).then_inc(oT_low, 1)

                    def add_direct(q):
                        n = QT[q][1]
                        dve.wait_ge(direct_ready, ev(f, 2, q))
                        dve.wait_ge(bias_added, ev(f, 2, q))
                        dve.scalar_tensor_tensor(xf[0:n, q, :], bank(q, n), gate[0:n, :], xf[0:n, q, :],
                                                 ALU.mult, ALU.add).then_inc(direct_added, 1)

                    if now:
                        maxes(0)
                    if tail:
                        dve.wait_ge(rstd2, ev(t, 1))
                        if not isinstance(s, int) or t >= 1:
                            dve.wait_ge(halves_out, 32 * t)
                            dve.wait_ge(xn2T_ready, ev(t - 1, 2, 1))
                        for q, (_, n) in enumerate(QT):
                            dve.tensor_scalar(xn2[0:n, q, :], xt[0:n, q, :], mv2[0:n, q, 0:1], rs2[0:n, q:q + 1],
                                              ALU.subtract, ALU.mult).then_inc(xn2_ready, 1)
                    if nxt:
                        for h in range(2):
                            low_pair(xnTL, xnTH, "xnT", f, 2, h, xnT_high, xnT_low)
                    if tail:
                        for q, (_, n) in enumerate(QT):
                            dve.wait_ge(half_high, ev(t, 2, q))
                            dve.wait_ge(xn2_ready, ev(t, 2, q))
                            dve.scalar_tensor_tensor(parts(halves[0:n, q, 1, :]), by_part(xn2[0:n, q, :]), UP, parts(halves[0:n, q, 0, :]),
                                                     ALU.mult, ALU.subtract).then_inc(half_low, 1)
                    if now:
                        maxes(1)
                    if nxt:
                        at_lows(0)
                        for q, (_, n) in enumerate(QT):
                            dve.wait_ge(xn_ready, ev(f, 2, q))
                            if q:
                                dve.wait_ge(keydot, ev(f, 2, q - 1))
                            dve.tensor_tensor_reduce(out=dot_junk[0:n, :], in0=xn[0:n, q, :], in1=key_bias_row[0:n, :],
                                                     scale=1.0, scalar=0.0, op0=ALU.mult, op1=ALU.add,
                                                     accum_out=kb[0:n, q, 0:1]).then_inc(keydot, 1)
                        at_lows(1)
                        for q, (_, n) in enumerate(QT):
                            dve.wait_ge(keydot, ev(f, 2, q))
                            dve.tensor_scalar(kb[0:n, q, 1:2], kb[0:n, q, 0:1], key_bias_const[0:n, :], None, ALU.add).then_inc(keybias, 1)
                    if now:
                        for n in range(3):
                            low_pair(pTL, pTH, "pT", s, 3, n, pT_high, pT_low, KP)
                    if nxt:
                        ctxT_lows(range(1))
                        add_direct(0)
                    if tail:
                        dve.wait_ge(logits_ready, ev(t, 1))
                        _, bk = ring("logits", 0)
                        dve.scalar_tensor_tensor(logits[:, 0, :, :], bank(bk, P, Q).rearrange("p (n t) -> p n t", t=G), bc[:, 0:1],
                                                 tie[:, :, :], ALU.add, ALU.add).then_inc(logits_read, 1)
                        dve.wait_ge(logits_read, ev(t, 1))
                        dve.tensor_reduce(best[:, :], logits[:, 0, :, :], AX.X, ALU.max).then_inc(best_found, 1)
                        dve.wait_ge(best_found, ev(t, 1))
                        dve.tensor_tensor(permT_all[:, bass.ds(t * Q, Q)].rearrange("p (n t) -> p n t", t=G), logits[:, 0, :, :],
                                          best[:, :].unsqueeze(2).broadcast_to([P, NB, G]), ALU.is_equal).then_inc(perm_ready, 1)
                    if nxt:
                        ctxT_lows(range(1, 4))
                    if now:
                        for q, (_, n) in enumerate(QT):
                            dve.wait_ge(probs_ready, ev(s, 2, q))
                            dve.reciprocal(share[0:n, q, 0:1], total[0:n, q:q + 1]).then_inc(recip, 1)
                        for q, (_, n) in enumerate(QT):
                            dve.wait_ge(recip, ev(s, 2, q))
                            dve.tensor_scalar(share[0:n, q, 1:2], share[0:n, q, 0:1], gate[0:n, :], None, ALU.mult).then_inc(share_ready, 1)
                        oT_lows(0)
                    if nxt:
                        ctxT_lows(range(4, 8))
                    if after:
                        dve.wait_ge(xn_in, 32 * g + 32)
                        for q, (_, n) in enumerate(QT):
                            dve.bn_stats(st1[0:n, q, :], xn[0:n, q, :]).then_inc(stats1, 1)
                        for q, (_, n) in enumerate(QT):
                            wait_apart(dve, stats1, ev(g, 2, q), passed_dve)
                            dve.bn_aggr(mv1[0:n, q, :], st1[0:n, q, :]).then_inc(meanvar1, 1)
                    if now:
                        oT_lows(1)
                    if after:
                        dve.wait_ge(rstd1, ev(g, 1))
                        for q, (_, n) in enumerate(QT):
                            dve.tensor_scalar(xn[0:n, q, :], xn[0:n, q, :], mv1[0:n, q, 0:1], rs1[0:n, q:q + 1],
                                              ALU.subtract, ALU.mult).then_inc(xn_ready, 1)
                    if nxt:
                        add_direct(1)

                steps(dve, one)

            @block.tensor
            def _(pe):
                def three(out, lhs, rhs, first, last):
                    (lh, ll), (rh, rl) = lhs, rhs
                    pe.matmul(out, lh, rl, start=first, stop=False)
                    pe.matmul(out, ll, rh, start=False, stop=False)
                    return pe.matmul(out, lh, rh, start=False, stop=last)

                def ctx_turn(f, s, par, ns):
                    for n in ns:
                        wait_ring(pe, s, "ctxT", n)
                        _, bk = ring("ctxT", n)
                        for j in range(3):
                            c = n % 2 * 3 + j
                            mm = pe.transpose(bank(bk)[:, j * KP:(j + 1) * KP], ctx_raw[1 - par][:, c, n // 2 * P:(n // 2 + 1) * P],
                                              ident[0:KP, 0:KP])
                        mm.then_inc(ctxT_ready, 1)

                def turn_tokens(src, kind, s, done):
                    for h in range(2):
                        wait_ring(pe, s, kind, h)
                        _, bk = ring(kind, h)
                        for d in (2 * h, 2 * h + 1):
                            for q, (q0, n) in enumerate(QT):
                                mm = pe.transpose(bank(bk)[:, d % 2 * Q + q0:d % 2 * Q + q0 + n], src[0:n, q, d * P:(d + 1) * P],
                                                  ident[0:n, 0:n])
                        mm.then_inc(done, 1)

                def one(s, par):
                    tail, now, nxt, _ = flags(s)
                    t, f = s - 1, s + 1

                    def scores(q):
                        q0, n = QT[q]
                        for h in range(2):
                            k0 = h * (K - KW)
                            for d in range(DT):
                                mm = three(bank(2 * q + h, n, KW), [w[:, d, q0:q0 + n] for w in (atH, atL)],
                                           [w[:, d, k0:k0 + KW] for w in (ctxTH, ctxTL)], d == 0, d == DT - 1)
                        mm.then_inc(scores_ready, 1)

                    def queries(h):
                        for m in (2 * h, 2 * h + 1):
                            for d in range(DT):
                                mm = three(bank(h)[:, m % 2 * Q:m % 2 * Q + Q], [w[:, d, m * P:(m + 1) * P] for w in (qkH, qkL)],
                                           [w[:, d, :] for w in (xnTH, xnTL)], d == 0, d == DT - 1)
                        mm.then_inc(at_ready, 1)

                    def sums(h):
                        for m in (2 * h, 2 * h + 1):
                            for c in range(KC):
                                mm = three(bank(2 + h)[:, m % 2 * Q:m % 2 * Q + Q], [w[:, c, m * P:(m + 1) * P] for w in (ctxH, ctxL)],
                                           [w[:, c, :] for w in (pTH, pTL)], c == 0, c == KC - 1)
                        mm.then_inc(oT_ready, 1)

                    def out_tile(bk, q, lhs, rhs, done):
                        q0, n = QT[q]
                        for d in range(DT):
                            mm = three(bank(bk, n), [w[:, d, q0:q0 + n] for w in lhs], [w[:, d, :] for w in rhs], d == 0, d == DT - 1)
                        mm.then_inc(done, 1)

                    if now:
                        pe.wait_ge(at_low, ev(s, 2, 1))
                        pe.wait_ge(ctxT_low, ev(s, 8, 7))
                        pe.wait_ge(direct_added, ev(s, 2, 1))
                        scores(0)
                    if nxt:
                        pe.wait_ge(xn_ready, ev(f, 2, 1))
                        turn_tokens(xn, "xnT", s, xnT_ready)
                    if now:
                        if tail:
                            pe.wait_ge(attended_added, ev(t, 2, 1))
                        scores(1)
                    if nxt:
                        pe.wait_ge(xnT_low, ev(f, 2, 1))
                        if now:
                            pe.wait_ge(probs_ready, ev(s, 2, 0))
                        queries(0)
                    if tail:
                        pe.wait_ge(xn2_ready, ev(t, 2, 1))
                        turn_tokens(xn2, "xn2T", s, xn2T_ready)
                    if nxt:
                        queries(1)
                    if now:
                        pe.wait_ge(probs_ready, ev(s, 2, 1))
                        for n in range(3):
                            wait_ring(pe, s, "pT", n)
                            _, bk = ring("pT", n)
                            for j, c in enumerate((2 * n, 2 * n + 1)):
                                for q, (q0, rows) in enumerate(QT):
                                    mm = pe.transpose(bank(bk, KP)[:, j * Q + q0:j * Q + q0 + rows],
                                                      probs[0:rows, q, c * KP:(c + 1) * KP], ident[0:rows, 0:rows])
                            mm.then_inc(pT_ready, 1)
                    if nxt:
                        pe.wait_ge(ctx_in[1 - par], ctx_arrived(f, 1 - par))
                        ctx_turn(f, s, par, range(1))
                        pe.wait_ge(at_low, ev(f, 2, 0))
                        out_tile(0, 0, (xnTH, xnTL), (woH, woL), direct_ready)
                    if tail:
                        pe.wait_ge(xn2T_copied, ev(t, 2, 1))
                        wait_ring(pe, s, "logits", 0)
                        _, bk = ring("logits", 0)
                        for d in range(DT):
                            mm = pe.matmul(bank(bk, P, Q), wc[:, d, :], xn2T[:, d, :], start=(d == 0), stop=(d == DT - 1))
                        mm.then_inc(logits_ready, 1)
                    if nxt:
                        ctx_turn(f, s, par, range(1, 4))
                    if now:
                        pe.wait_ge(pT_low, ev(s, 3, 2))
                        pe.wait_ge(ctx_low, ev(s, KC, KC - 1))
                        sums(0)
                    if nxt:
                        ctx_turn(f, s, par, range(4, 8))
                    if now:
                        sums(1)
                    if nxt:
                        pe.wait_ge(at_low, ev(f, 2, 1))
                        out_tile(1, 1, (xnTH, xnTL), (woH, woL), direct_ready)
                    if now:
                        pe.wait_ge(oT_low, ev(s, 2, 1))
                        for q in range(2):
                            out_tile(2 + q, q, (oTH, oTL), (wvoH, wvoL), attended_ready)

                steps(pe, one)


def make_masks(nc, pool, pieces, made):
    pool.memset(pieces[:, :], 1.0).then_inc(made, 1)
    pool.wait_ge(made, 1)
    pool.affine_select(out=pieces[:, :], in_=pieces[:, :], compare_op=ALU.is_ge, fill=0.0,
                       base=0, pattern=[[-32, 4]], channel_multiplier=1).then_inc(made, 1)
    pool.wait_ge(made, 2)
    pool.affine_select(out=pieces[:, :], in_=pieces[:, :], compare_op=ALU.is_ge, fill=0.0,
                       base=31, pattern=[[32, 4]], channel_multiplier=-1).then_inc(made, 1)


def experts_up(nc, sh, a, scratch, permT_all):
    ES, F, N, DT, C = sh.ES, sh.F, sh.N, sh.DT, sh.C
    TT = sh.T // P
    NJ = ES // 4
    JB = 4
    BLKS = NJ // JB
    EB = 4 * JB
    FT = max(n for n in range(1, 9) if TT % n == 0)
    FILLS = TT // FT
    PER = FILLS * DT
    GP = P // sh.G
    w1_v = a["L0_ffn_W1"].rearrange("(r g) s (p t) f -> p r (g s) (t f)", r=4, t=DT)
    tok_v = scratch["halves"].rearrange("b q h d -> (b q) h d").rearrange("(t p) h d -> p t h d", p=P)

    with ExitStack() as es:
        def sb(name, shape, dt=F32):
            return es.enter_context(nc.sbuf_tensor(name, shape, dt))

        def sem(name):
            return es.enter_context(nc.semaphore(name))

        tok = sb("tok", [P, TT, 2, C], F16)
        perm = sb("perm", [P, TT, ES], F16)
        pick = [sb(f"pick{n}", [P, TT, EB, GP], F16) for n in range(2)]
        chosen = [sb(f"chosen{n}", [P, EB, N]) for n in range(2)]
        w1 = [sb(f"w1_{n}", [P, 4, JB, DT, F]) for n in range(2)]
        hidden = [sb(f"hidden{n}", [P, JB, N]) for n in range(2)]
        b1 = sb("b1", [P, NJ])
        ident = sb("ident16", [P, P], F16)
        pieces = sb("pieces", [P, 4], F16)
        ps = es.enter_context(nc.psum_tensor("ps_up", [P, 8, BANK], F32))

        tok_in = [sem(f"tok_in{n}") for n in range(FILLS)]
        w1_in = [sem(f"w1_in{n}") for n in range(2)]
        b1_in = sem("b1_in")
        masks = sem("masks_made")
        ident_made = sem("ident16_made")
        perm_turned, perm_copied = sem("perm_turned"), sem("perm_copied")
        pick_made = sem("pick_made")
        gathered, up_done = sem("gathered"), sem("up_done")
        moved = [sem("chosen_by_act"), sem("chosen_by_dve")]
        hidden_made, hidden_out = sem("hidden_made"), [sem(f"hidden_out{n}") for n in range(2)]

        def blocks(eng, one):
            one(0, 0)
            one(1, 1)
            with eng.Fori(1, BLKS // 2) as m:
                one(2 * m, 0)
                one(2 * m + 1, 1)

        def first(k, upto=0):
            return isinstance(k, int) and k <= upto

        def share(f, eng):
            return (f + 1) // 2 if eng == 0 else f // 2

        with nc.Block() as block:
            @block.sync
            def _(sp):
                for f in range(FILLS):
                    sp.dma_start(tok[:, f * FT:(f + 1) * FT, :, :], tok_v[:, f * FT:(f + 1) * FT, :, :]).then_inc(tok_in[f], 16)
                with nc.allow_non_contiguous_dma(reason="b1 as columns"):
                    b1_v = a["L0_ffn_b1"].rearrange("(r g) s f -> r f (g s)", r=4)
                    for r in range(4):
                        sp.dma_start(b1[r * F:(r + 1) * F, :], b1_v[r]).then_inc(b1_in, 16)

                def one(k, par):
                    if not first(k, 1):
                        sp.wait_ge(up_done, ev(k - 2, DT, DT - 1))
                    for r in range(4):
                        sp.dma_start(w1[par][:, r, :, :, :].rearrange("p j t f -> p j (t f)"),
                                     w1_v[:, r, bass.ds(k * JB, JB), :]).then_inc(w1_in[par], 16)
                    if not first(k):
                        store(k - 1, 1 - par)

                def store(k, par):
                    sp.wait_ge(hidden_made, ev(k, JB, JB - 1))
                    sp.dma_start(scratch["hidden"][bass.ds(k * JB, JB)].rearrange("j p n -> p j n"), hidden[par][:, :, :]).then_inc(hidden_out[par], 16)

                blocks(sp, one)
                store(BLKS - 1, 1)
                for n in range(2):
                    sp.wait_ge(hidden_out[n], 16 * (BLKS // 2))

            @block.gpsimd
            def _(pool):
                make_masks(nc, pool, pieces, masks)
                pool.memset(ident[:, :], 0.0).then_inc(ident_made, 1)
                pool.wait_ge(ident_made, 1)
                pool.affine_select(out=ident[:, :], in_=ident[:, :], compare_op=ALU.not_equal, fill=1.0,
                                   base=0, pattern=[[-1, P]], channel_multiplier=1).then_inc(ident_made, 1)
                pool.wait_ge(masks, 3)

                def one(k, par):
                    for f in range(FILLS):
                        if first(k):
                            pool.wait_ge(perm_copied, min((f + 1) * FT, TT))
                        if not first(k, 1):
                            pool.wait_ge(gathered, ev(k - 2, PER, (DT - 1) * FILLS + f))
                        ts = slice(f * FT, (f + 1) * FT)
                        pool.tensor_tensor(pick[par][:, ts, :, :], perm[:, ts, bass.ds(k * EB, EB)].unsqueeze(3).broadcast_to([P, FT, EB, GP]),
                                           pieces[:, :].unsqueeze(1).unsqueeze(1).broadcast_to([P, FT, EB, GP]), ALU.mult).then_inc(pick_made, 1)

                blocks(pool, one)

            def evacuate(eng, which, k, parts):
                for t in parts:
                    for f in range(FILLS):
                        n = t * FILLS + f
                        if n % 2 != which:
                            continue
                        if f <= 1 and not (first(k) and t < 2):
                            eng.wait_ge(up_done, ev(k, DT, t - 2) if t >= 2 else ev(k - 1, DT, t + 2))
                        eng.wait_ge(gathered, ev(k, PER, n))
                        dst = chosen[t % 2][:, :, f * FT * GP:(f + 1) * FT * GP].rearrange("p e (t n) -> p t e n", n=GP)
                        src = ps[:, n % 4, 0:FT * EB * GP].rearrange("p (t e n) -> p t e n", t=FT, e=EB)
                        if which == 0:
                            eng.activation(dst, src, ACT.Copy, scale=1.0 / UP).then_inc(moved[0], 1)
                        else:
                            eng.tensor_scalar(dst, src, 1.0 / UP, None, ALU.mult).then_inc(moved[1], 1)

            @block.scalar
            def _(act):
                act.wait_ge(b1_in, 64)

                def one(k, par):
                    evacuate(act, 0, k, range(1))
                    if not first(k):
                        relu(k - 1, 1 - par)
                    evacuate(act, 0, k, range(1, DT))

                def relu(k, par):
                    act.wait_ge(up_done, ev(k, DT, DT - 1))
                    if not first(k, 1):
                        act.wait_ge(hidden_out[par], 8 * (k - par))
                    for j in range(JB):
                        act.activation(hidden[par][:, j, :], ps[:, 4 + j, 0:N], ACT.Relu,
                                       bias=b1[:, bass.ds(k * JB + j, 1)]).then_inc(hidden_made, 1)

                blocks(act, one)
                relu(BLKS - 1, 1)

            @block.vector
            def _(dve):
                for t in range(TT):
                    dve.wait_ge(perm_turned, t + 1)
                    src = ps[:, 4 + t % 4, 0:P // 2].bitcast(F16).rearrange("p (r k j) -> p r k j", r=4, j=JB)
                    dst = perm[:, t, :].rearrange("p (k r j) -> p r k j", r=4, j=JB)
                    dve.tensor_copy(dst, src).then_inc(perm_copied, 1)

                def one(k, par):
                    evacuate(dve, 1, k, range(DT))

                blocks(dve, one)

            @block.tensor
            def _(pe):
                pe.wait_ge(ident_made, 2)
                for t in range(TT):
                    if t >= 4:
                        pe.wait_ge(perm_copied, t - 3)
                    pe.transpose(ps[:, 4 + t % 4, 0:P // 2].bitcast(F16), permT_all[:, t * P:(t + 1) * P], ident[:, :]).then_inc(perm_turned, 1)

                def gather(k, par, t):
                    for f in range(FILLS):
                        n = t * FILLS + f
                        if first(k) and t == 0:
                            pe.wait_ge(tok_in[f], 16)
                        if t == 0:
                            pe.wait_ge(pick_made, ev(k, FILLS, f))
                        if n >= 4:
                            pe.wait_ge(moved[n % 2], share_value(k, n - 4))
                        elif not first(k):
                            pe.wait_ge(moved[n % 2], share_value(k - 1, PER + n - 4))
                        for i in range(FT):
                            tt = f * FT + i
                            out = ps[:, n % 4, i * EB * GP:(i + 1) * EB * GP]
                            rhs = pick[par][:, tt, :, :].rearrange("p e n -> p (e n)")
                            for h in (1, 0):
                                mm = pe.matmul(out, tok[:, tt, h, t * P:(t + 1) * P], rhs, start=(h == 1), stop=(h == 0))
                        mm.then_inc(gathered, 1)

                def share_value(k, n):
                    return ev(k, PER // 2, n // 2)

                def up(k, par, t):
                    n = (t + 1) * FILLS - 1
                    for m in (n, n - 1):
                        pe.wait_ge(moved[m % 2], share_value(k, m))
                    if t == 0:
                        pe.wait_ge(w1_in[par], 32 * (k - par) + 64)
                        if not first(k):
                            pe.wait_ge(hidden_made, ev(k - 1, JB, JB - 1))
                        else:
                            pe.wait_ge(perm_copied, TT)
                    for j in range(JB):
                        for r in range(4):
                            mm = pe.matmul(ps[r * F:(r + 1) * F, 4 + j, 0:N], w1[par][:, r, j, t, :], chosen[t % 2][:, r * JB + j, :],
                                           start=(t == 0), stop=(t == DT - 1))
                    mm.then_inc(up_done, 1)

                def one(k, par):
                    for t in range(DT):
                        gather(k, par, t)
                        if t > 0:
                            up(k, par, t - 1)
                        elif not first(k):
                            up(k - 1, 1 - par, DT - 1)

                blocks(pe, one)
                up(BLKS - 1, 1, DT - 1)


def experts_down(nc, sh, a, scratch, permT_all, out):
    ES, F, N, DT, C, G = sh.ES, sh.F, sh.N, sh.DT, sh.C, sh.G
    NJ = ES // 4
    GB = 32
    NBLK = N // GB
    TB = GB * G
    JG = 4
    QW = C // 4
    HW = C // 2
    FQ = NJ // JG
    RING = 4
    TILES = TB // P
    SLOTS = 16
    w2_v = a["L0_ffn_W2"].rearrange("g s (p t) f -> p (g s) (t f)", t=DT)
    x2_v = scratch["x2"].rearrange("b q d -> (b q) d")
    out_v = out.rearrange("b q d -> (b q) d")
    hid_v = scratch["hidden"].rearrange("j p n -> p j n")

    with ExitStack() as es:
        def sb(name, shape, dt=F32):
            return es.enter_context(nc.sbuf_tensor(name, shape, dt))

        def sem(name):
            return es.enter_context(nc.semaphore(name))

        w2T = sb("w2T", [P, NJ, C])
        answers = sb("answers", [P, 2, GB, HW])
        w2_raw = answers[:, :, :, :].rearrange("p h n d -> p (h n d)").rearrange("p (e t f) -> p e t f", t=DT, f=F)
        stage = sb("stage", [P, 2, NJ, QW])
        w2_group = stage[:, :, :, :].rearrange("p q j d -> p (q j d)").rearrange("p (s c) -> p s c", s=SLOTS)
        hid = sb("hid", [P, NJ, GB])
        wide = sb("hidden_wide", [P, NJ, 4, GB])
        permR = sb("permR", [P, TB], F32R)
        b2H, b2L = (sb(f"b2{h}", [P, C], F32R) for h in "HL")
        XB = 4
        x2 = sb("x2_tiles", [P, XB, HW])
        b2 = x2[:, 0:2, :].rearrange("p a d -> p (a d)")
        ident = sb("ident32", [P, P])
        pieces = sb("pieces32", [P, 4])
        g_raw, gate = sb("g2_raw", [P, 1]), sb("gate2", [P, 1])
        ps = es.enter_context(nc.psum_tensor("ps_down", [P, 8, BANK], F32))

        CH = 8
        w2_in = [sem(f"w2_in{n}") for n in range(CH)]
        small = sem("small_in")
        masks, ident_made, gate_done = sem("masks32_made"), sem("ident32_made"), sem("gate2_done")
        w2_grouped, w2_turned = sem("w2_grouped"), sem("w2_turned")
        w2_copied = [sem("w2_by_act"), sem("w2_by_dve")]
        b2_high, b2_low = sem("b2_high"), sem("b2_low")
        hid_in = sem("hid_in")
        wide_made = sem("wide_hidden_made")
        down, staged, turned = sem("down_done"), sem("staged"), sem("answers_turned")
        perm_cast = sem("perm_cast")
        summed, added = sem("summed"), sem("added")
        x2_in, x2_out = [sem(f"x2_in{n}") for n in range(XB)], [sem(f"x2_out{n}") for n in range(XB)]

        def known(k):
            return isinstance(k, int)

        def blocks(eng, one):
            one(0)
            one(1)
            with eng.Fori(2, NBLK - 1) as k:
                one(k)
            one(NBLK - 1)
            one(NBLK)

        def parts(k):
            return (k < NBLK, k >= 1) if known(k) else (True, True)

        def tile(k, h, i):
            return (2 * k + h) * TILES + i

        with nc.Block() as block:
            @block.sync
            def _(sp):
                for n in range(CH):
                    w = NJ // CH
                    for r in range(4):
                        e0 = r * NJ + n * w
                        sp.dma_start(w2_raw[:, e0:e0 + w, :, :].rearrange("p e t f -> p e (t f)"), w2_v[:, e0:e0 + w, :]).then_inc(w2_in[n], 16)
                sp.dma_start(b2, a["L0_ffn_b2"].rearrange("g s d -> (g s) d")).then_inc(small, 16)
                sp.dma_start(g_raw[:, :], a["g_ffn"].rearrange("(o c) -> o c", o=1).broadcast_to([P, 1])).then_inc(small, 16)
                sp.dma_start(hid[:, :, :], hid_v[:, :, 0:GB]).then_inc(hid_in, 16)

                def rows(v, k, h, i):
                    return v[bass.ds(k * TB + i * P, P), h * HW:(h + 1) * HW]

                def load(k, h, i):
                    i, h, k = (i + 2, h, k) if i + 2 < TILES else (i + 2 - TILES, 1 - h, k + h)
                    if known(k) and k >= NBLK:
                        return
                    if not (known(k) and tile(k, h, i) < XB):
                        sp.wait_ge(x2_out[i % XB], 16 * ev(2 * k + h, TILES // XB, i // XB - 1))
                    sp.dma_start(x2[:, i % XB, :], rows(x2_v, k, h, i)).then_inc(x2_in[i % XB], 16)

                def tiles(k, h):
                    for i in range(TILES):
                        sp.wait_ge(added, ev(tile(k, h, i), 1))
                        sp.dma_start(rows(out_v, k, h, i), x2[:, i % XB, :]).then_inc(x2_out[i % XB], 16)
                        load(k, h, i)

                sp.wait_ge(b2_low, 1)
                for i in range(2):
                    sp.dma_start(x2[:, i, :], rows(x2_v, 0, 0, i)).then_inc(x2_in[i], 16)

                def one(k):
                    here, before = parts(k)
                    if before and (not known(k) or k < NBLK):
                        sp.wait_ge(wide_made, ev(k - 1, FQ, FQ - 1))
                        sp.dma_start(hid[:, :, :], hid_v[:, :, bass.ds(k * GB, GB)]).then_inc(hid_in, 16)
                    if before:
                        tiles(k - 1, 1)
                    if here:
                        tiles(k, 0)

                blocks(sp, one)
                for b in range(XB):
                    sp.wait_ge(x2_out[b], 16 * NBLK * 2 * TILES // XB)

            @block.gpsimd
            def _(pool):
                make_masks(nc, pool, pieces, masks)
                pool.memset(ident[:, :], 0.0).then_inc(ident_made, 1)
                pool.wait_ge(ident_made, 1)
                pool.affine_select(out=ident[:, :], in_=ident[:, :], compare_op=ALU.not_equal, fill=1.0,
                                   base=0, pattern=[[-1, P]], channel_multiplier=1).then_inc(ident_made, 1)
                pool.wait_ge(masks, 3)
                for j in range(NJ):
                    pool.wait_ge(w2_in[j * CH // NJ], 64)
                    if j >= SLOTS:
                        pool.wait_ge(w2_turned, j - SLOTS + 1)
                    pool.tensor_copy(w2_group[:, j % SLOTS, :].rearrange("p (t r f) -> p t r f", t=DT, r=4),
                                     w2_raw[:, j:ES:NJ, :, :].rearrange("p r t f -> p t r f")).then_inc(w2_grouped, 1)

                def one(k):
                    if not parts(k)[0]:
                        return
                    pool.wait_ge(hid_in, 16 * ev(k, 1))
                    for g in range(FQ):
                        if not (known(k) and k == 0):
                            pool.wait_ge(down, ev(k - 1, 4 * FQ, 3 * FQ + g))
                        at = slice(g * JG, (g + 1) * JG)
                        pool.tensor_tensor(wide[:, at, :, :], hid[:, at, :].unsqueeze(2).broadcast_to([P, JG, 4, GB]),
                                           pieces[:, :].unsqueeze(1).unsqueeze(3).broadcast_to([P, JG, 4, GB]), ALU.mult).then_inc(wide_made, 1)

                blocks(pool, one)

            def copy_w2(eng, which):
                for j in range(which, NJ, 2):
                    eng.wait_ge(w2_turned, j + 1)
                    dst = w2T[:, j, :].rearrange("p (q t) -> p q t", t=DT)
                    src = ps[:, j % RING, :].rearrange("p (t q) -> p q t", t=DT)
                    if which == 0:
                        eng.activation(dst, src, ACT.Copy).then_inc(w2_copied[0], 1)
                    else:
                        eng.tensor_copy(dst, src).then_inc(w2_copied[1], 1)

            @block.scalar
            def _(act):
                act.wait_ge(small, 32)
                act.activation(gate[:, :], g_raw[:, :], ACT.Tanh).then_inc(gate_done, 1)
                act.activation(b2H[:, :], b2, ACT.Copy).then_inc(b2_high, 1)
                copy_w2(act, 0)
                act.wait_ge(w2_turned, NJ)

                def one(k):
                    here, _ = parts(k)
                    if not here:
                        return
                    for q in range(4):
                        for g in range(FQ):
                            act.wait_ge(down, ev(k, 4 * FQ, q * FQ + g))
                            if g == 0 and not (known(k) and k == 0 and q < 2):
                                act.wait_ge(turned, ev(k, 4, q - 2) if q >= 2 else ev(k - 1, 4, q + 2))
                            act.activation(stage[:, q % 2, g * JG:(g + 1) * JG, :], ps[:, g % RING, :].rearrange("p (j d) -> p j d", j=JG),
                                           ACT.Copy).then_inc(staged, 1)
                        if q == 1:
                            if not (known(k) and k == 0):
                                act.wait_ge(summed, ev(tile(k - 1, 1, TILES - 1), 1))
                            act.activation(permR[:, :], permT_all[:, bass.ds(k * TB, TB)], ACT.Copy).then_inc(perm_cast, 1)

                blocks(act, one)

            @block.vector
            def _(dve):
                dve.wait_ge(small, 32)
                dve.wait_ge(b2_high, 1)
                dve.tensor_tensor(b2L[:, :], b2, b2H[:, :].bitcast(F32), ALU.subtract).then_inc(b2_low, 1)
                copy_w2(dve, 1)
                dve.wait_ge(gate_done, 1)
                dve.wait_ge(w2_grouped, NJ)

                def turn(k, q):
                    dve.wait_ge(staged, ev(k, 4 * FQ, q * FQ + FQ - 1))
                    if q % 2 == 0 and not (known(k) and k == 0):
                        dve.wait_ge(summed, ev(tile(k - 1, q // 2, TILES - 1), 1))
                    at = slice(q % 2 * QW, q % 2 * QW + QW)
                    dve.transpose(answers[:, q // 2, :, at].rearrange("p n d -> p d n"),
                                  stage[:, q % 2, :, :].rearrange("p j d -> p d j")).then_inc(turned, 1)

                def add(k, h):
                    for i in range(TILES):
                        dve.wait_ge(summed, ev(tile(k, h, i), 1))
                        dve.wait_ge(x2_in[i % XB], 16 * ev(2 * k + h, TILES // XB, i // XB))
                        xt = x2[:, i % XB, :]
                        dve.scalar_tensor_tensor(xt, ps[:, RING + i % RING, 0:HW], gate[:, 0:1], xt, ALU.mult, ALU.add).then_inc(added, 1)

                def one(k):
                    here, before = parts(k)
                    if here:
                        turn(k, 0)
                    if before:
                        add(k - 1, 1)
                    if here:
                        turn(k, 1)
                        turn(k, 2)
                        add(k, 0)
                        turn(k, 3)

                blocks(dve, one)

            @block.tensor
            def _(pe):
                pe.wait_ge(ident_made, 2)
                for j in range(NJ):
                    if j >= RING:
                        pe.wait_ge(w2_copied[j % 2], (j - RING) // 2 + 1)
                    pe.wait_ge(w2_grouped, j + 1)
                    for t in range(DT):
                        mm = pe.transpose(ps[:, j % RING, t * P:(t + 1) * P],
                                          w2_group[:, j % SLOTS, t * P:(t + 1) * P], ident[:, :])
                    mm.then_inc(w2_turned, 1)
                pe.wait_ge(b2_low, 1)
                pe.wait_ge(w2_copied[0], NJ // 2)
                pe.wait_ge(w2_copied[1], NJ // 2)

                def downs(k, q):
                    for g in range(FQ):
                        if q == 0:
                            pe.wait_ge(wide_made, ev(k, FQ, g))
                        n = q * FQ + g
                        if n >= RING:
                            pe.wait_ge(staged, ev(k, 4 * FQ, n - RING))
                        elif not (known(k) and k == 0):
                            pe.wait_ge(staged, ev(k - 1, 4 * FQ, 4 * FQ + n - RING))
                        for i in range(JG):
                            j = g * JG + i
                            mm = pe.matmul(ps[:, g % RING, i * QW:(i + 1) * QW], wide[:, j, :, :].rearrange("p r n -> p (r n)"),
                                           w2T[:, j, q * QW:(q + 1) * QW], start=True, stop=True)
                        mm.then_inc(down, 1)

                def sums(k, h):
                    pe.wait_ge(turned, ev(k, 4, 2 * h + 1))
                    if h == 0:
                        pe.wait_ge(perm_cast, ev(k, 1))
                    for i in range(TILES):
                        n = tile(k, h, i)
                        if not (known(n) and n < RING):
                            pe.wait_ge(added, ev(n - RING, 1))
                        acc = ps[:, RING + i % RING, 0:HW]
                        who = permR[:, i * P:(i + 1) * P]
                        at = slice(h * HW, (h + 1) * HW)
                        pe.matmul(acc, who, b2H[:, at], start=True, stop=False)
                        pe.matmul(acc, who, b2L[:, at], start=False, stop=False)
                        for g in range(P // G):
                            mm = pe.matmul(acc[g * G:(g + 1) * G, :], who[:, g * G:(g + 1) * G].bitcast(F32),
                                           answers[:, h, i * (P // G) + g, :], start=False, stop=True)
                        mm.then_inc(summed, 1)

                def one(k):
                    here, before = parts(k)
                    if here:
                        downs(k, 0)
                    if before:
                        sums(k - 1, 1)
                    if here:
                        downs(k, 1)
                        downs(k, 2)
                        sums(k, 0)
                        downs(k, 3)

                blocks(pe, one)


def flamingo_gated(nc, a, out):
    sh = Shapes(a["x"], a["ctx_1024"], a["L0_ffn_Wc"], a["L0_ffn_W1"])
    scratch = {
        "x2": nc.dram_tensor("x2_scratch", [sh.B, sh.Q, sh.C], F32, kind="Internal").ap(),
        "halves": nc.dram_tensor("halves_scratch", [sh.B, sh.Q, 2, sh.C], F16, kind="Internal").ap(),
        "hidden": nc.dram_tensor("hidden_scratch", [sh.ES // 4, P, sh.N], F32, kind="Internal").ap(),
    }
    with nc.sbuf_tensor("permT_all", [P, sh.T], F16) as permT_all:
        attention_and_routing(nc, sh, a, scratch, permT_all)
        experts_up(nc, sh, a, scratch, permT_all)
        experts_down(nc, sh, a, scratch, permT_all, out)


_INS = ["x", "ctx_1024", "g_xattn", "g_ffn", "L0_xattn_Wq", "L0_xattn_bq", "L0_xattn_Wk", "L0_xattn_bk", "L0_xattn_Wv",
        "L0_xattn_bv", "L0_xattn_Wo", "L0_xattn_bo", "L0_ffn_Wc", "L0_ffn_bc", "L0_ffn_W1", "L0_ffn_b1", "L0_ffn_W2", "L0_ffn_b2"]


def kernel(**inputs):
    import numpy as _np
    import concourse.bacc as _bacc
    from concourse import mybir as _mybir
    from concourse.bass_utils import run_bass_kernel_spmd as _run

    nc = _bacc.Bacc("TRN2", target_bir_lowering=False, num_devices=1)
    arrays, aps = {}, {}
    for name in _INS:
        v = _np.ascontiguousarray(inputs[name])
        arrays[f"in_{name}"] = v
        aps[name] = nc.dram_tensor(f"in_{name}", v.shape, _mybir.dt.from_np(v.dtype), kind="ExternalInput").ap()
    out = nc.dram_tensor("out", inputs["x"].shape, _mybir.dt.float32, kind="ExternalOutput").ap()
    flamingo_gated(nc, aps, out)
    r = _run(nc, [arrays], core_ids=[0])
    return r.results[0]["out"]
```

```python
import concourse.bass as bass
from concourse import mybir
from contextlib import ExitStack
import numpy as np

F32 = mybir.dt.float32
F32R = mybir.dt.float32r
F16 = mybir.dt.float16
ALU = mybir.AluOpType
ACT = mybir.ActivationFunctionType
AX = mybir.AxisListType

P = 128
BANK = 512
EPS = 1e-5
UP = 256.0
TIE = 1e-6


def ev(index, per, k=0):
    return per * index + k + 1


class Shapes:

    def __init__(self, x, ctx, wc, w1):
        self.B, self.Q, self.C = x.shape
        self.K = ctx.shape[1]
        self.G, self.S = wc.shape[1:]
        self.ES = self.G * self.S
        self.F = w1.shape[3]
        self.DT = self.C // P
        self.QT = [(0, P), (P, self.Q - P)]
        self.KP = 125
        self.KC = self.K // self.KP
        self.NB = self.Q // self.G
        self.T = self.B * self.Q
        self.N = self.T // self.G


def wait_apart(eng, sem, value, passed):
    eng.wait_ge(sem, value)
    eng.sem_inc(passed, 1)


def attention_and_routing(nc, sh, a, scratch, permT_all):
    B, Q, C, K, DT, KP, KC, QT = sh.B, sh.Q, sh.C, sh.K, sh.DT, sh.KP, sh.KC, sh.QT
    G, NB, ES = sh.G, sh.NB, sh.ES
    SCALE = float(C) ** -0.5
    KH = K // 2
    KW = KH + KH % 2
    x_d, ctx_d = a["x"], a["ctx_1024"]
    ctx_v = ctx_d.rearrange("b (p c) d -> b p c d", c=KC)

    with ExitStack() as es:
        def sb(name, shape, dt=F32):
            return es.enter_context(nc.sbuf_tensor(name, shape, dt))

        def sem(name):
            return es.enter_context(nc.semaphore(name))

        qkH, qkL = (sb(f"w_qk{h}", [P, DT, C], F32R) for h in "HL")
        woH, woL = (sb(f"w_o{h}", [P, DT, C], F32R) for h in "HL")
        wvoH, wvoL = (sb(f"w_vo{h}", [P, DT, C], F32R) for h in "HL")
        qk_bias = sb("qk_bias", [P, DT])
        key_bias_row = sb("key_bias_row", [P, C])
        key_bias_const = sb("key_bias_const", [P, 1])
        out_bias_row = sb("out_bias_row", [P, C])
        gate = sb("gate", [P, 1])
        wc = sb("wc", [P, DT, ES])
        bc = sb("bc", [P, 1])
        tie = sb("tie", [P, NB, G])
        ident = sb("ident", [P, P])
        minus_half = sb("minus_half", [P, 2])
        mv1, mv2 = (sb(f"mean_var{n}", [P, 2, 2]) for n in (1, 2))

        ctx_raw = [sb(f"ctx_raw{p}", [KP, KC, C]) for p in range(2)]
        x = [sb(f"x{p}", [P, 2, C]) for p in range(2)]
        xn = sb("xn", [P, 2, C])
        ctx_in = [sem(f"ctx_in{p}") for p in range(2)]
        x_in = [sem(f"x_in{p}") for p in range(2)]
        xn_in = sem("xn_in")
        st1 = sb("bn_stats1", [P, 2, 6])
        ve1, rs1 = sb("var_eps1", [P, 2]), sb("rstd1", [P, 2])
        stats1, meanvar1, vareps1, rstd1, xn_ready = (sem(n) for n in ("stats1", "meanvar1", "vareps1", "rstd1", "xn_ready"))
        passed_dve, passed_pool = sem("passed_by_dve"), sem("passed_by_pool")

        def load_x(sp, b, par):
            for q, (q0, n) in enumerate(QT):
                sp.dma_start(x[par][0:n, q, :], x_d[b, q0:q0 + n, :]).then_inc(x_in[par], 16)

        def load_xn(sp, b):
            for q, (q0, n) in enumerate(QT):
                sp.dma_start(xn[0:n, q, :], x_d[b, q0:q0 + n, :]).then_inc(xn_in, 16)

        def load_ctx(sp, b, par):
            sp.dma_start(ctx_raw[par][:, :, :], ctx_v[b]).then_inc(ctx_in[par], 16)

        def x_stats(dve, b):
            dve.wait_ge(xn_in, 32 * b + 32)
            for q, (_, n) in enumerate(QT):
                dve.bn_stats(st1[0:n, q, :], xn[0:n, q, :]).then_inc(stats1, 1)
            for q, (_, n) in enumerate(QT):
                wait_apart(dve, stats1, ev(b, 2, q), passed_dve)
                dve.bn_aggr(mv1[0:n, q, :], st1[0:n, q, :]).then_inc(meanvar1, 1)

        def x_normalise(dve, b):
            dve.wait_ge(rstd1, ev(b, 1))
            for q, (_, n) in enumerate(QT):
                dve.tensor_scalar(xn[0:n, q, :], xn[0:n, q, :], mv1[0:n, q, 0:1], rs1[0:n, q:q + 1],
                                  ALU.subtract, ALU.mult).then_inc(xn_ready, 1)

        def rstd(pool, b, meanvar, mv, ve, vareps, rs, rs_sem):
            wait_apart(pool, meanvar, ev(b, 2, 1), passed_pool)
            pool.tensor_scalar(ve[:, :], mv[:, :, 1], EPS, 1.0, ALU.add, ALU.mult).then_inc(vareps, 1)
            wait_apart(pool, vareps, ev(b, 1), passed_pool)
            pool.tensor_tensor(rs[:, :], ve[:, :], minus_half[:, 0:2], ALU.pow).then_inc(rs_sem, 1)

        def weights():
            with ExitStack() as ws:
                def wb(name, shape, dt=F32):
                    return ws.enter_context(nc.sbuf_tensor(name, shape, dt))

                def wsem(name):
                    return ws.enter_context(nc.semaphore(name))

                raw = {n: wb(f"raw_{n}", [P, DT, C]) for n in ("Wq", "Wk", "Wv", "Wo")}
                split = {n: [wb(f"{n}_{h}", [P, DT, C], F32R) for h in "HL"] for n in ("Wq", "Wk", "Wv")}
                cols = wb("bias_cols", [P, 3, DT])
                wide = wb("bias_wide", [P, 2, DT, P])
                woT = wb("woT", [P, DT, C])
                bo_row = wb("bo_row", [P, C])
                g_raw = wb("g_raw", [P, 1])
                ps = ws.enter_context(nc.psum_tensor("ps_weights", [P, 8, BANK], F32))
                qk_loaded = [wsem(f"Wq_Wk_loaded{h}") for h in range(DT)]
                loaded = {n: wsem(f"{n}_loaded") for n in ("Wo", "Wv")}
                small = wsem("small_loaded")
                iota = wsem("constants_made")
                wide_made = wsem("wide_made")
                turned = wsem("wo_turned")
                turned_copied = wsem("wo_turned_copied")
                product = wsem("product_ready")
                split_high, split_low = wsem("weight_high_made"), wsem("weight_low_made")
                high = wsem("high_half_made")
                low = wsem("low_half_made")
                rows = wsem("row_ready")
                rows_out = wsem("row_copied")
                gate_done = wsem("gate_done")
                summed = wsem("bias_summed")

                with nc.Block() as block:
                    @block.sync
                    def _(sp):
                        for h in range(DT):
                            for n in ("Wq", "Wk"):
                                sp.dma_start(raw[n][:, h, :], a[f"L0_xattn_{n}"][h * P:(h + 1) * P, :]).then_inc(qk_loaded[h], 16)
                        for n in ("Wo", "Wv"):
                            sp.dma_start(raw[n][:, :, :], a[f"L0_xattn_{n}"].rearrange("(t p) c -> p t c", p=P)).then_inc(loaded[n], 16)
                        for n, name in enumerate(("bq", "bk", "bv")):
                            with nc.allow_non_contiguous_dma(reason="a bias as columns"):
                                sp.dma_start(cols[:, n, :], a[f"L0_xattn_{name}"].rearrange("(t p) -> p t", p=P)).then_inc(small, 16)
                        sp.dma_start(bo_row[:, :], a["L0_xattn_bo"].rearrange("(o c) -> o c", o=1).broadcast_to([P, C])).then_inc(small, 16)
                        sp.dma_start(g_raw[:, :], a["g_xattn"].rearrange("(o c) -> o c", o=1).broadcast_to([P, 1])).then_inc(small, 16)
                        sp.dma_start(wc[:, :, :], a["L0_ffn_Wc"].rearrange("(t p) e s -> p t (e s)", p=P)).then_inc(small, 16)
                        with nc.allow_non_contiguous_dma(reason="a bias as a column"):
                            sp.dma_start(bc[:, :], a["L0_ffn_bc"].rearrange("e (s o) -> (e s) o", o=1)).then_inc(small, 16)
                        load_xn(sp, 0)
                        load_ctx(sp, 0, 0)
                        load_x(sp, 0, 0)
                        load_ctx(sp, 1, 1)
                        load_x(sp, 1, 1)

                    @block.gpsimd
                    def _(pool):
                        pool.memset(ident[:, :], 0.0).then_inc(iota, 1)
                        pool.memset(minus_half[:, :], -0.5).then_inc(iota, 1)
                        pool.wait_ge(iota, 2)
                        pool.affine_select(out=ident[:, :], in_=ident[:, :], compare_op=ALU.not_equal, fill=1.0,
                                           base=0, pattern=[[-1, P]], channel_multiplier=1).then_inc(iota, 1)
                        for mv in (mv1, mv2):
                            pool.memset(mv[:, :, :], 0.0).then_inc(iota, 1)
                        ties = np.linspace(0.0, TIE, G, dtype=np.float32)
                        for t in range(G):
                            pool.memset(tie[:, :, t], float(ties[t])).then_inc(iota, 1)
                        rstd(pool, 0, meanvar1, mv1, ve1, vareps1, rs1, rstd1)

                    @block.tensor
                    def _(pe):
                        def product_of(bank, lhs, rhs, t):
                            (lh, ll), (rh, rl) = lhs, rhs
                            at = slice(t * P, (t + 1) * P)
                            for h in range(DT):
                                if lhs is split["Wq"] and t == 0:
                                    pe.wait_ge(split_low, 2 * (h + 1))
                                pe.matmul(ps[:, bank, :], lh[:, h, at], rl[:, h, :], start=(h == 0), stop=False)
                                pe.matmul(ps[:, bank, :], ll[:, h, at], rh[:, h, :], start=False, stop=False)
                                mm = pe.matmul(ps[:, bank, :], lh[:, h, at], rh[:, h, :], start=False, stop=(h == DT - 1))
                            mm.then_inc(product, 1)

                        for t in range(DT):
                            product_of(4 + t, split["Wq"], split["Wk"], t)
                        pe.wait_ge(iota, 3)
                        pe.wait_ge(loaded["Wo"], 16)
                        for t in range(DT):
                            for o in range(DT):
                                mm = pe.transpose(ps[:, t, o * P:(o + 1) * P], raw["Wo"][:, o, t * P:(t + 1) * P], ident[:, :])
                            mm.then_inc(turned, 1)
                        pe.wait_ge(wide_made, 2)
                        pe.wait_ge(low, DT)
                        for h in range(DT):
                            mm = pe.matmul(ps[:, 5, :], wide[:, 1, h, :], raw["Wq"][:, h, :], start=(h == 0), stop=(h == DT - 1))
                        mm.then_inc(rows, 1)
                        for t in range(DT):
                            for h in range(DT):
                                mm = pe.matmul(ps[:, 6, t:t + 1], raw["Wk"][:, h, t * P:(t + 1) * P], cols[:, 0, h:h + 1],
                                               start=(h == 0), stop=(h == DT - 1))
                        mm.then_inc(rows, 1)
                        for h in range(DT):
                            mm = pe.matmul(ps[:, 7, 0:1], wide[:, 1, h, :], cols[:, 0, h:h + 1], start=(h == 0), stop=(h == DT - 1))
                        mm.then_inc(rows, 1)
                        pe.wait_ge(turned_copied, DT)
                        for h in range(DT):
                            mm = pe.matmul(ps[:, 4, :], wide[:, 0, h, :], woT[:, h, :], start=(h == 0), stop=(h == DT - 1))
                        mm.then_inc(rows, 1)
                        pe.wait_ge(split_low, 3 * DT)
                        pe.wait_ge(low, 2 * DT)
                        for t in range(DT):
                            product_of(t, split["Wv"], (woH, woL), t)

                    @block.scalar
                    def _(act):
                        def product_highs(dst, first, bank):
                            for t in range(DT):
                                act.wait_ge(product, first + t + 1)
                                act.activation(dst[:, t, :], ps[:, bank + t, :], ACT.Copy).then_inc(high, 1)

                        for h in range(DT):
                            act.wait_ge(qk_loaded[h], 32)
                            for name in ("Wq", "Wk"):
                                act.activation(split[name][0][:, h, :], raw[name][:, h, :], ACT.Copy).then_inc(split_high, 1)
                        act.wait_ge(loaded["Wv"], 16)
                        for h in range(DT):
                            act.activation(split["Wv"][0][:, h, :], raw["Wv"][:, h, :], ACT.Copy).then_inc(split_high, 1)
                        act.wait_ge(small, 16 * 7)
                        act.activation(gate[:, :], g_raw[:, :], ACT.Tanh).then_inc(gate_done, 1)
                        product_highs(qkH, 0, 4)
                        for t in range(DT):
                            act.wait_ge(turned, t + 1)
                            act.activation(woH[:, t, :], ps[:, t, :], ACT.Copy).then_inc(high, 1)
                        product_highs(wvoH, DT, 0)

                    @block.vector
                    def _(dve):
                        def product_lows(hi, lo, first, bank):
                            for t in range(DT):
                                dve.wait_ge(high, first + t + 1)
                                dve.tensor_tensor(lo[:, t, :], ps[:, bank + t, :], hi[:, t, :].bitcast(F32), ALU.subtract).then_inc(low, 1)

                        in_order = [(name, h) for h in range(DT) for name in ("Wq", "Wk")] + [("Wv", h) for h in range(DT)]
                        for number, (name, h) in enumerate(in_order):
                            hi, lo = split[name]
                            dve.wait_ge(split_high, number + 1)
                            dve.tensor_tensor(lo[:, h, :], raw[name][:, h, :], hi[:, h, :].bitcast(F32), ALU.subtract).then_inc(split_low, 1)
                        dve.wait_ge(small, 16 * 7)
                        for n, col in enumerate((2, 1)):
                            dve.tensor_copy(wide[:, n, :, :], cols[:, col, :].unsqueeze(2).broadcast_to([P, DT, P])).then_inc(wide_made, 1)
                        product_lows(qkH, qkL, 0, 4)
                        for t in range(DT):
                            dve.wait_ge(high, DT + t + 1)
                            dve.tensor_copy(woT[:, t, :], ps[:, t, :]).then_inc(turned_copied, 1)
                            dve.wait_ge(turned_copied, t + 1)
                            dve.tensor_tensor(woL[:, t, :], woT[:, t, :], woH[:, t, :].bitcast(F32), ALU.subtract).then_inc(low, 1)
                        dve.wait_ge(rows, 4)
                        dve.tensor_tensor(out_bias_row[:, :], ps[:, 4, :], bo_row[:, :], ALU.add).then_inc(summed, 1)
                        dve.wait_ge(summed, 1)
                        dve.wait_ge(gate_done, 1)
                        dve.tensor_scalar(out_bias_row[:, :], out_bias_row[:, :], gate[:, :], None, ALU.mult).then_inc(rows_out, 1)
                        dve.tensor_copy(key_bias_row[:, :], ps[:, 5, :]).then_inc(rows_out, 1)
                        dve.tensor_copy(qk_bias[:, :], ps[:, 6, 0:DT]).then_inc(rows_out, 1)
                        dve.tensor_copy(key_bias_const[:, :], ps[:, 7, 0:1]).then_inc(rows_out, 1)
                        dve.wait_ge(iota, 5)
                        x_stats(dve, 0)
                        x_normalise(dve, 0)
                        product_lows(wvoH, wvoL, 2 * DT, 0)

        weights()

        ctxH, ctxL = (sb(f"ctx{h}", [KP, KC, C], F32R) for h in "HL")
        ctxTH, ctxTL = (sb(f"ctxT{h}", [P, DT, K], F32R) for h in "HL")
        xnTH, xnTL = (sb(f"xnT{h}", [P, DT, Q], F32R) for h in "HL")
        atH, atL = (sb(f"at{h}", [P, DT, Q], F32R) for h in "HL")
        probs = sb("probs", [P, 2, K])
        pTH, pTL = (sb(f"probsT{h}", [KP, KC, Q], F32R) for h in "HL")
        oTH, oTL = (sb(f"oT{h}", [P, DT, Q], F32R) for h in "HL")
        xn2 = sb("xn2", [P, 2, C])
        dot_junk = sb("dot_junk", [P, C], F16)
        halves = sb("token_halves", [P, 2, DT, 2, P], F16)
        xn2T = sb("xn2T", [P, DT, Q])
        logits = sb("logits", [P, NB, G])
        st2 = sb("bn_stats2", [P, 2, 6])
        ve2, rs2 = sb("var_eps2", [P, 2]), sb("rstd2", [P, 2])
        kb = sb("query_key_bias", [P, 2, 2])
        top = sb("row_max", [P, 2])
        shift = sb("exp_shift", [P, 2, 2])
        total = sb("prob_sum", [P, 2])
        share = sb("gate_over_sum", [P, 2, 2])
        best = sb("best_logit", [P, NB])
        ps = es.enter_context(nc.psum_tensor("ps", [P, 8 * BANK], F32))

        x_out = [sem(f"x_out{p}") for p in range(2)]
        halves_out = sem("halves_out")
        ctxT_ready, ctxT_high, ctxT_low = sem("ctxT_ready"), sem("ctxT_high"), sem("ctxT_low")
        xnT_ready, xnT_high, xnT_low = sem("xnT_ready"), sem("xnT_high"), sem("xnT_low")
        at_ready, at_high, at_low = sem("at_ready"), sem("at_high"), sem("at_low")
        scores_ready, probs_ready = sem("scores_ready"), sem("probs_ready")
        pT_ready, pT_high, pT_low = sem("pT_ready"), sem("pT_high"), sem("pT_low")
        oT_ready, oT_high, oT_low = sem("oT_ready"), sem("oT_high"), sem("oT_low")
        direct_ready, direct_added = sem("direct_ready"), sem("direct_added")
        attended_ready, attended_added = sem("attended_ready"), sem("attended_added")
        xn2T_ready, xn2T_copied = sem("xn2T_ready"), sem("xn2T_copied")
        logits_ready, logits_read = sem("logits_ready"), sem("logits_read")
        ctx_high, ctx_low = sem("ctx_high"), sem("ctx_low")
        stats2, meanvar2, vareps2, rstd2, xn2_ready = (sem(n) for n in ("stats2", "meanvar2", "vareps2", "rstd2", "xn2_ready"))
        keydot, keybias = sem("keydot"), sem("keybias")
        bias_added = sem("bias_added")
        rowmax, shift_part, shift_ready = sem("rowmax"), sem("shift_part"), sem("shift_ready")
        recip, share_ready = sem("recip"), sem("share_ready")
        half_high, half_low = sem("half_high"), sem("half_low")
        best_found, perm_ready = sem("best_found"), sem("perm_ready")

        def by_part(v):
            return v.rearrange("n (p t) -> n t p", t=DT)

        def bank(n, rows=P, cols=BANK):
            return ps[0:rows, n * BANK:n * BANK + cols]

        FILLS = ([("xnT", n, 1) for n in range(2)] + [("xn2T", n, -1) for n in range(2)] + [("pT", n, 0) for n in range(3)]
                 + [("ctxT", 0, 1), ("logits", 0, -1)] + [("ctxT", n, 1) for n in range(1, 8)])
        FREED = {"xn2T": (xn2T_copied, 2), "ctxT": (ctxT_low, 8), "logits": (logits_read, 1), "pT": (pT_low, 3), "xnT": (xnT_low, 2)}

        def ring(kind, n):
            at = next(f for f, (k, m, _) in enumerate(FILLS) if (k, m) == (kind, n))
            return at, 4 + at % 4

        def exists(step, batch_off):
            if not isinstance(step, int):
                return True
            return 0 <= step + batch_off < B

        def wait_ring(pe, step, kind, n):
            at, _ = ring(kind, n)
            back = 0
            while True:
                at -= 4
                if at < 0:
                    at, back = at + len(FILLS), back + 1
                k, m, off = FILLS[at]
                if isinstance(step, int) and step - back < -1:
                    return
                if not isinstance(step, int) or exists(step - back, off):
                    freed, per = FREED[k]
                    pe.wait_ge(freed, ev(step - back + off, per, m))
                    return

        def steps(eng, one):
            one(-1, 1)
            one(0, 0)
            if B > 2:
                one(1, 1)
            pairs = max((B - 4) // 2, 0)
            if pairs:
                with eng.Fori(1, 1 + pairs) as m:
                    one(2 * m, 0)
                    one(2 * m + 1, 1)
            for s in range(2 + 2 * pairs, B - 1):
                one(s, s % 2)
            one(B - 1, (B - 1) % 2)
            one(B, B % 2)

        def flags(s):
            if not isinstance(s, int):
                return True, True, True, True
            return s >= 1, 0 <= s < B, 0 <= s + 1 < B, s + 2 < B

        def ctx_arrived(b, par):
            return 8 * (b - par) + 16

        def x_arrived(b, par):
            return 16 * (b - par) + 32

        def score_view(q):
            n = QT[q][1]
            at = 2 * q * BANK
            skip = BANK + KW - KH
            return ps[0:n, at:at + 2 * skip].rearrange("p (a b) -> p a b", b=skip)[:, :, 0:KH]

        with nc.Block() as block:
            @block.sync
            def _(sp):
                def one(s, par):
                    tail, now, nxt, after = flags(s)
                    if tail:
                        t = s - 1
                        o = 1 - par
                        for q, (q0, n) in enumerate(QT):
                            sp.wait_ge(attended_added, ev(t, 2, q))
                            sp.dma_start(scratch["x2"][t, q0:q0 + n, :], x[o][0:n, q, :]).then_inc(x_out[o], 16)
                    if now and after:
                        sp.wait_ge(ctxT_ready, ev(s, 8, 7))
                        sp.wait_ge(ctx_low, ev(s, KC, KC - 1))
                        load_ctx(sp, s + 2, par)
                    if tail and nxt:
                        sp.wait_ge(x_out[o], 16 * (t - o) + 32)
                        sp.wait_ge(xn2_ready, ev(t, 2, 1))
                        load_x(sp, s + 1, o)
                    if tail:
                        for q, (q0, n) in enumerate(QT):
                            sp.wait_ge(half_low, ev(t, 2, q))
                            sp.dma_start(scratch["halves"][t, q0:q0 + n], halves[0:n, q, :, :, :]).then_inc(halves_out, 16)
                    if nxt and after:
                        sp.wait_ge(xnT_ready, ev(s + 1, 2, 1))
                        sp.wait_ge(keydot, ev(s + 1, 2, 1))
                        load_xn(sp, s + 2)
                    if isinstance(s, int) and s == B:
                        for o in range(2):
                            sp.wait_ge(x_out[o], 32 * (B // 2 if B % 2 == 0 else (B + 1 - o) // 2))
                        sp.wait_ge(halves_out, 32 * B)

                steps(sp, one)

            @block.gpsimd
            def _(pool):
                def one(s, par):
                    tail, now, nxt, after = flags(s)

                    if tail:
                        rstd(pool, s - 1, meanvar2, mv2, ve2, vareps2, rs2, rstd2)
                    if nxt:
                        pool.wait_ge(x_in[1 - par], x_arrived(s + 1, 1 - par))
                        for q, (_, n) in enumerate(QT):
                            xv = x[1 - par][0:n, q, :]
                            pool.tensor_tensor(xv, xv, out_bias_row[0:n, :], ALU.add).then_inc(bias_added, 1)
                    if after:
                        rstd(pool, s + 2, meanvar1, mv1, ve1, vareps1, rs1, rstd1)
                    if nxt:
                        for c in range(KC):
                            pool.wait_ge(ctx_high, ev(s + 1, KC, c))
                            pool.tensor_tensor(ctxL[:, c, :], ctx_raw[1 - par][:, c, :], ctxH[:, c, :].bitcast(F32),
                                               ALU.subtract).then_inc(ctx_low, 1)

                steps(pool, one)

            @block.scalar
            def _(act):
                def one(s, par):
                    tail, now, nxt, _ = flags(s)
                    t, f = s - 1, s + 1

                    def exps(q):
                        n = QT[q][1]
                        act.wait_ge(shift_ready, ev(s, 2, q))
                        if not isinstance(s, int) or s >= 1:
                            act.wait_ge(pT_ready, ev(s - 1, 3, 2))
                        act.activation(probs[0:n, q, :].rearrange("p (a b) -> p a b", b=KH), score_view(q),
                                       ACT.Exp, bias=shift[0:n, q, 1:2], scale=SCALE,
                                       accum_out=total[0:n, q:q + 1]).then_inc(probs_ready, 1)

                    def high_pair(dst, kind, b, per, n, ready, done, rows=P):
                        act.wait_ge(ready, ev(b, per, n))
                        _, bk = ring(kind, n)
                        act.activation(dst[:, 2 * n:2 * n + 2, :], bank(bk, rows, 2 * Q).rearrange("p (a q) -> p a q", a=2),
                                       ACT.Copy).then_inc(done, 1)

                    def at_highs(h):
                        act.wait_ge(at_ready, ev(f, 2, h))
                        for m in (2 * h, 2 * h + 1):
                            act.activation(atH[:, m, :], bank(h)[:, m % 2 * Q:m % 2 * Q + Q], ACT.Identity,
                                           bias=qk_bias[:, m:m + 1]).then_inc(at_high, 1)

                    def ctxT_highs(ns):
                        for n in ns:
                            act.wait_ge(ctxT_ready, ev(f, 8, n))
                            _, bk = ring("ctxT", n)
                            act.activation(ctxTH[:, n // 2, n % 2 * KH:n % 2 * KH + KH], bank(bk, P, KH), ACT.Copy).then_inc(ctxT_high, 1)

                    def oT_highs(h):
                        act.wait_ge(oT_ready, ev(s, 2, h))
                        act.activation(oTH[:, 2 * h:2 * h + 2, :], bank(2 + h, P, 2 * Q).rearrange("p (a q) -> p a q", a=2),
                                       ACT.Copy).then_inc(oT_high, 1)

                    if now:
                        exps(0)
                    if nxt:
                        if now:
                            act.wait_ge(direct_ready, ev(f - 1, 2, 1))
                        for h in range(2):
                            high_pair(xnTH, "xnT", f, 2, h, xnT_ready, xnT_high)
                    if tail:
                        if not isinstance(s, int) or t >= 1:
                            act.wait_ge(halves_out, 32 * t)
                        for q, (_, n) in enumerate(QT):
                            act.wait_ge(xn2_ready, ev(t, 2, q))
                            act.activation(halves[0:n, q, :, 0, :], by_part(xn2[0:n, q, :]), ACT.Copy, scale=UP).then_inc(half_high, 1)
                    if now:
                        exps(1)
                    if nxt:
                        at_highs(0)
                    if tail:
                        for h in range(2):
                            high_pair(xn2T, "xn2T", t, 2, h, xn2T_ready, xn2T_copied)
                    if nxt:
                        at_highs(1)
                    if now:
                        if not isinstance(s, int) or s >= 1:
                            act.wait_ge(oT_ready, ev(s - 1, 2, 1))
                        for n in range(3):
                            high_pair(pTH, "pT", s, 3, n, pT_ready, pT_high, KP)
                    if nxt:
                        if now:
                            act.wait_ge(scores_ready, ev(s, 2, 1))
                        ctxT_highs(range(4))
                    if now:
                        if not isinstance(s, int) or s >= 1:
                            act.wait_ge(attended_ready, ev(s - 1, 2, 1))
                        oT_highs(0)
                    if nxt:
                        ctxT_highs(range(4, 8))
                    if now:
                        oT_highs(1)
                    if nxt:
                        act.wait_ge(ctx_in[1 - par], ctx_arrived(f, 1 - par))
                        for c in range(KC):
                            act.activation(ctxH[:, c, :], ctx_raw[1 - par][:, c, :], ACT.Copy).then_inc(ctx_high, 1)

                steps(act, one)

            @block.vector
            def _(dve):
                def one(s, par):
                    tail, now, nxt, after = flags(s)
                    t, f, g = s - 1, s + 1, s + 2
                    xt = xf = x[1 - par]
                    if tail:
                        for q, (_, n) in enumerate(QT):
                            dve.wait_ge(attended_ready, ev(t, 2, q))
                            dve.wait_ge(direct_added, ev(t, 2, q))
                            dve.wait_ge(share_ready, ev(t, 2, q))
                            dve.scalar_tensor_tensor(xt[0:n, q, :], bank(2 + q, n), share[0:n, q, 1:2], xt[0:n, q, :],
                                                     ALU.mult, ALU.add).then_inc(attended_added, 1)
                            dve.wait_ge(attended_added, ev(t, 2, q))
                            dve.bn_stats(st2[0:n, q, :], xt[0:n, q, :]).then_inc(stats2, 1)
                        for q, (_, n) in enumerate(QT):
                            wait_apart(dve, stats2, ev(t, 2, q), passed_dve)
                            dve.bn_aggr(mv2[0:n, q, :], st2[0:n, q, :]).then_inc(meanvar2, 1)

                    def maxes(q):
                        n = QT[q][1]
                        dve.wait_ge(scores_ready, ev(s, 2, q))
                        dve.tensor_reduce(top[0:n, q:q + 1], score_view(q), AX.XY, ALU.max).then_inc(rowmax, 1)
                        dve.wait_ge(rowmax, ev(s, 2, q))
                        dve.wait_ge(keybias, ev(s, 2, q))
                        dve.tensor_scalar(shift[0:n, q, 0:1], top[0:n, q:q + 1], kb[0:n, q, 1:2], -SCALE, ALU.add, ALU.mult).then_inc(shift_part, 1)
                        dve.wait_ge(shift_part, ev(s, 2, q))
                        dve.scalar_tensor_tensor(shift[0:n, q, 1:2], kb[0:n, q, 1:2], SCALE, shift[0:n, q, 0:1],
                                                 ALU.mult, ALU.add).then_inc(shift_ready, 1)

                    def low_pair(lo, hi, kind, b, per, n, high, done, rows=P):
                        dve.wait_ge(high, ev(b, per, n))
                        _, bk = ring(kind, n)
                        at = slice(2 * n, 2 * n + 2)
                        dve.tensor_tensor(lo[:, at, :], bank(bk, rows, 2 * Q).rearrange("p (a q) -> p a q", a=2),
                                          hi[:, at, :].bitcast(F32), ALU.subtract).then_inc(done, 1)

                    def at_lows(h):
                        dve.wait_ge(at_high, ev(f, 4, 2 * h + 1))
                        for m in (2 * h, 2 * h + 1):
                            ins = dve.scalar_tensor_tensor(atL[:, m, :], bank(h)[:, m % 2 * Q:m % 2 * Q + Q], qk_bias[:, m:m + 1],
                                                           atH[:, m, :].bitcast(F32), ALU.add, ALU.subtract)
                        ins.then_inc(at_low, 1)

                    def ctxT_lows(ns):
                        for n in ns:
                            dve.wait_ge(ctxT_high, ev(f, 8, n))
                            _, bk = ring("ctxT", n)
                            at = slice(n % 2 * KH, n % 2 * KH + KH)
                            dve.tensor_tensor(ctxTL[:, n // 2, at], bank(bk, P, KH), ctxTH[:, n // 2, at].bitcast(F32),
                                              ALU.subtract).then_inc(ctxT_low, 1)

                    def oT_lows(h):
                        dve.wait_ge(oT_high, ev(s, 2, h))
                        at = slice(2 * h, 2 * h + 2)
                        dve.tensor_tensor(oTL[:, at, :], bank(2 + h, P, 2 * Q).rearrange("p (a q) -> p a q", a=2),
                                          oTH[:, at, :].bitcast(F32), ALU.subtract).then_inc(oT_low, 1)

                    def add_direct(q):
                        n = QT[q][1]
                        dve.wait_ge(direct_ready, ev(f, 2, q))
                        dve.wait_ge(bias_added, ev(f, 2, q))
                        dve.scalar_tensor_tensor(xf[0:n, q, :], bank(q, n), gate[0:n, :], xf[0:n, q, :],
                                                 ALU.mult, ALU.add).then_inc(direct_added, 1)

                    if now:
                        maxes(0)
                    if tail:
                        dve.wait_ge(rstd2, ev(t, 1))
                        if not isinstance(s, int) or t >= 1:
                            dve.wait_ge(halves_out, 32 * t)
                            dve.wait_ge(xn2T_ready, ev(t - 1, 2, 1))
                        for q, (_, n) in enumerate(QT):
                            dve.tensor_scalar(xn2[0:n, q, :], xt[0:n, q, :], mv2[0:n, q, 0:1], rs2[0:n, q:q + 1],
                                              ALU.subtract, ALU.mult).then_inc(xn2_ready, 1)
                    if nxt:
                        for h in range(2):
                            low_pair(xnTL, xnTH, "xnT", f, 2, h, xnT_high, xnT_low)
                    if tail:
                        for q, (_, n) in enumerate(QT):
                            dve.wait_ge(half_high, ev(t, 2, q))
                            dve.wait_ge(xn2_ready, ev(t, 2, q))
                            dve.scalar_tensor_tensor(halves[0:n, q, :, 1, :], by_part(xn2[0:n, q, :]), UP, halves[0:n, q, :, 0, :],
                                                     ALU.mult, ALU.subtract).then_inc(half_low, 1)
                    if now:
                        maxes(1)
                    if nxt:
                        at_lows(0)
                        for q, (_, n) in enumerate(QT):
                            dve.wait_ge(xn_ready, ev(f, 2, q))
                            if q:
                                dve.wait_ge(keydot, ev(f, 2, q - 1))
                            dve.tensor_tensor_reduce(out=dot_junk[0:n, :], in0=xn[0:n, q, :], in1=key_bias_row[0:n, :],
                                                     scale=1.0, scalar=0.0, op0=ALU.mult, op1=ALU.add,
                                                     accum_out=kb[0:n, q, 0:1]).then_inc(keydot, 1)
                        at_lows(1)
                        for q, (_, n) in enumerate(QT):
                            dve.wait_ge(keydot, ev(f, 2, q))
                            dve.tensor_scalar(kb[0:n, q, 1:2], kb[0:n, q, 0:1], key_bias_const[0:n, :], None, ALU.add).then_inc(keybias, 1)
                    if now:
                        for n in range(3):
                            low_pair(pTL, pTH, "pT", s, 3, n, pT_high, pT_low, KP)
                    if nxt:
                        ctxT_lows(range(1))
                        add_direct(0)
                    if tail:
                        dve.wait_ge(logits_ready, ev(t, 1))
                        _, bk = ring("logits", 0)
                        dve.scalar_tensor_tensor(logits[:, :, :], bank(bk, P, Q).rearrange("p (n t) -> p n t", t=G), bc[:, 0:1],
                                                 tie[:, :, :], ALU.add, ALU.add).then_inc(logits_read, 1)
                        dve.wait_ge(logits_read, ev(t, 1))
                        dve.tensor_reduce(best[:, :], logits[:, :, :], AX.X, ALU.max).then_inc(best_found, 1)
                        dve.wait_ge(best_found, ev(t, 1))
                        dve.tensor_tensor(permT_all[:, bass.ds(t * Q, Q)].rearrange("p (n t) -> p n t", t=G), logits[:, :, :],
                                          best[:, :].unsqueeze(2).broadcast_to([P, NB, G]), ALU.is_equal).then_inc(perm_ready, 1)
                    if nxt:
                        ctxT_lows(range(1, 4))
                    if now:
                        for q, (_, n) in enumerate(QT):
                            dve.wait_ge(probs_ready, ev(s, 2, q))
                            dve.reciprocal(share[0:n, q, 0:1], total[0:n, q:q + 1]).then_inc(recip, 1)
                        for q, (_, n) in enumerate(QT):
                            dve.wait_ge(recip, ev(s, 2, q))
                            dve.tensor_scalar(share[0:n, q, 1:2], share[0:n, q, 0:1], gate[0:n, :], None, ALU.mult).then_inc(share_ready, 1)
                        oT_lows(0)
                    if nxt:
                        ctxT_lows(range(4, 8))
                    if after:
                        x_stats(dve, g)
                    if now:
                        oT_lows(1)
                    if nxt and not now:
                        add_direct(1)
                    if after:
                        x_normalise(dve, g)
                    if nxt and now:
                        add_direct(1)

                steps(dve, one)

            @block.tensor
            def _(pe):
                def three(out, lhs, rhs, first, last):
                    (lh, ll), (rh, rl) = lhs, rhs
                    pe.matmul(out, lh, rl, start=first, stop=False)
                    pe.matmul(out, ll, rh, start=False, stop=False)
                    return pe.matmul(out, lh, rh, start=False, stop=last)

                def ctx_turn(f, s, par, ns):
                    for n in ns:
                        wait_ring(pe, s, "ctxT", n)
                        _, bk = ring("ctxT", n)
                        for j in range(3):
                            c = n % 2 * 3 + j
                            mm = pe.transpose(bank(bk)[:, j * KP:(j + 1) * KP], ctx_raw[1 - par][:, c, n // 2 * P:(n // 2 + 1) * P],
                                              ident[0:KP, 0:KP])
                        mm.then_inc(ctxT_ready, 1)

                def turn_tokens(src, kind, s, done):
                    for h in range(2):
                        wait_ring(pe, s, kind, h)
                        _, bk = ring(kind, h)
                        for d in (2 * h, 2 * h + 1):
                            for q, (q0, n) in enumerate(QT):
                                mm = pe.transpose(bank(bk)[:, d % 2 * Q + q0:d % 2 * Q + q0 + n], src[0:n, q, d * P:(d + 1) * P],
                                                  ident[0:n, 0:n])
                        mm.then_inc(done, 1)

                def one(s, par):
                    tail, now, nxt, _ = flags(s)
                    t, f = s - 1, s + 1

                    def scores(q):
                        q0, n = QT[q]
                        for h in range(2):
                            k0 = h * (K - KW)
                            for d in range(DT):
                                mm = three(bank(2 * q + h, n, KW), [w[:, d, q0:q0 + n] for w in (atH, atL)],
                                           [w[:, d, k0:k0 + KW] for w in (ctxTH, ctxTL)], d == 0, d == DT - 1)
                        mm.then_inc(scores_ready, 1)

                    def queries(h):
                        for m in (2 * h, 2 * h + 1):
                            for d in range(DT):
                                mm = three(bank(h)[:, m % 2 * Q:m % 2 * Q + Q], [w[:, d, m * P:(m + 1) * P] for w in (qkH, qkL)],
                                           [w[:, d, :] for w in (xnTH, xnTL)], d == 0, d == DT - 1)
                        mm.then_inc(at_ready, 1)

                    def sums(h):
                        for m in (2 * h, 2 * h + 1):
                            for c in range(KC):
                                mm = three(bank(2 + h)[:, m % 2 * Q:m % 2 * Q + Q], [w[:, c, m * P:(m + 1) * P] for w in (ctxH, ctxL)],
                                           [w[:, c, :] for w in (pTH, pTL)], c == 0, c == KC - 1)
                        mm.then_inc(oT_ready, 1)

                    def out_tile(bk, q, lhs, rhs, done):
                        q0, n = QT[q]
                        for d in range(DT):
                            mm = three(bank(bk, n), [w[:, d, q0:q0 + n] for w in lhs], [w[:, d, :] for w in rhs], d == 0, d == DT - 1)
                        mm.then_inc(done, 1)

                    if now:
                        pe.wait_ge(at_low, ev(s, 2, 1))
                        pe.wait_ge(ctxT_low, ev(s, 8, 7))
                        pe.wait_ge(direct_added, ev(s, 2, 1))
                        scores(0)
                    if nxt:
                        pe.wait_ge(xn_ready, ev(f, 2, 1))
                        turn_tokens(xn, "xnT", s, xnT_ready)
                    if now:
                        if tail:
                            pe.wait_ge(attended_added, ev(t, 2, 1))
                        scores(1)
                    if nxt:
                        pe.wait_ge(xnT_low, ev(f, 2, 1))
                        if now:
                            pe.wait_ge(probs_ready, ev(s, 2, 0))
                        queries(0)
                    if tail:
                        pe.wait_ge(xn2_ready, ev(t, 2, 1))
                        turn_tokens(xn2, "xn2T", s, xn2T_ready)
                    if nxt:
                        queries(1)
                    if now:
                        pe.wait_ge(probs_ready, ev(s, 2, 1))
                        for n in range(3):
                            wait_ring(pe, s, "pT", n)
                            _, bk = ring("pT", n)
                            for j, c in enumerate((2 * n, 2 * n + 1)):
                                for q, (q0, rows) in enumerate(QT):
                                    mm = pe.transpose(bank(bk, KP)[:, j * Q + q0:j * Q + q0 + rows],
                                                      probs[0:rows, q, c * KP:(c + 1) * KP], ident[0:rows, 0:rows])
                            mm.then_inc(pT_ready, 1)
                    if nxt:
                        pe.wait_ge(ctx_in[1 - par], ctx_arrived(f, 1 - par))
                        ctx_turn(f, s, par, range(1))
                        pe.wait_ge(at_low, ev(f, 2, 0))
                        out_tile(0, 0, (xnTH, xnTL), (woH, woL), direct_ready)
                    if tail:
                        pe.wait_ge(xn2T_copied, ev(t, 2, 1))
                        wait_ring(pe, s, "logits", 0)
                        _, bk = ring("logits", 0)
                        for d in range(DT):
                            mm = pe.matmul(bank(bk, P, Q), wc[:, d, :], xn2T[:, d, :], start=(d == 0), stop=(d == DT - 1))
                        mm.then_inc(logits_ready, 1)
                    if nxt:
                        ctx_turn(f, s, par, range(1, 4))
                    if now:
                        pe.wait_ge(pT_low, ev(s, 3, 2))
                        pe.wait_ge(ctx_low, ev(s, KC, KC - 1))
                        sums(0)
                    if nxt:
                        ctx_turn(f, s, par, range(4, 8))
                    if now:
                        sums(1)
                    if nxt:
                        pe.wait_ge(at_low, ev(f, 2, 1))
                        out_tile(1, 1, (xnTH, xnTL), (woH, woL), direct_ready)
                    if now:
                        pe.wait_ge(oT_low, ev(s, 2, 1))
                        for q in range(2):
                            out_tile(2 + q, q, (oTH, oTL), (wvoH, wvoL), attended_ready)

                steps(pe, one)


def make_masks(nc, pool, pieces, made):
    pool.memset(pieces[:, :], 1.0).then_inc(made, 1)
    pool.wait_ge(made, 1)
    pool.affine_select(out=pieces[:, :], in_=pieces[:, :], compare_op=ALU.is_ge, fill=0.0,
                       base=0, pattern=[[-32, 4]], channel_multiplier=1).then_inc(made, 1)
    pool.wait_ge(made, 2)
    pool.affine_select(out=pieces[:, :], in_=pieces[:, :], compare_op=ALU.is_ge, fill=0.0,
                       base=31, pattern=[[32, 4]], channel_multiplier=-1).then_inc(made, 1)


def experts_up(nc, sh, a, scratch, permT_all):
    ES, F, N, DT, C = sh.ES, sh.F, sh.N, sh.DT, sh.C
    TT = sh.T // P
    NJ = ES // 4
    JB = 4
    BLKS = NJ // JB
    EB = 4 * JB
    FT = max(n for n in range(1, 9) if TT % n == 0)
    FILLS = TT // FT
    PER = FILLS * DT
    GP = P // sh.G
    w1_v = a["L0_ffn_W1"].rearrange("(r g) s (p t) f -> p r (g s) (t f)", r=4, t=DT)
    tok_v = scratch["halves"].rearrange("b q t h d -> (b q) t (h d)").rearrange("(n p) t d -> p n t d", p=P)

    with ExitStack() as es:
        def sb(name, shape, dt=F32):
            return es.enter_context(nc.sbuf_tensor(name, shape, dt))

        def sem(name):
            return es.enter_context(nc.semaphore(name))

        tok = sb("tok", [P, TT, DT, 2, P], F16)
        perm = sb("perm", [P, TT, ES], F16)
        pick = [sb(f"pick{n}", [P, TT, EB, GP], F16) for n in range(2)]
        chosen = [sb(f"chosen{n}", [P, EB, N]) for n in range(2)]
        w1 = [sb(f"w1_{n}", [P, 4, JB, DT, F]) for n in range(2)]
        hidden = [sb(f"hidden{n}", [P, JB, N]) for n in range(2)]
        b1 = sb("b1", [P, NJ])
        ident = sb("ident16", [P, P], F16)
        pieces = sb("pieces", [P, 4], F16)
        ps = es.enter_context(nc.psum_tensor("ps_up", [P, 8, BANK], F32))

        first_part_in = [sem(f"tok_first_part_in{n}") for n in range(FILLS)]
        part_in = [None] + [sem(f"tok_part_in{t}") for t in range(1, DT)]
        w1_in = [sem(f"w1_in{n}") for n in range(2)]
        b1_in = sem("b1_in")
        choices_out = sem("choices_out")
        masks = sem("masks_made")
        ident_made = sem("ident16_made")
        perm_turned, perm_copied = sem("perm_turned"), sem("perm_copied")
        pick_made = sem("pick_made")
        gathered, up_done = sem("gathered"), sem("up_done")
        moved = [sem("chosen_by_act"), sem("chosen_by_dve")]
        hidden_made, hidden_out = sem("hidden_made"), [sem(f"hidden_out{n}") for n in range(2)]

        def blocks(eng, one):
            one(0, 0)
            one(1, 1)
            with eng.Fori(1, BLKS // 2) as m:
                one(2 * m, 0)
                one(2 * m + 1, 1)

        def first(k, upto=0):
            return isinstance(k, int) and k <= upto

        def share(f, eng):
            return (f + 1) // 2 if eng == 0 else f // 2

        with nc.Block() as block:
            @block.sync
            def _(sp):
                def load_tokens(t, n0, n1, done):
                    sp.dma_start(tok[:, n0:n1, t, :, :].rearrange("p n h d -> p n (h d)"), tok_v[:, n0:n1, t, :]).then_inc(done, 16)

                def load_w1(k, par):
                    for r in range(4):
                        sp.dma_start(w1[par][:, r, :, :, :].rearrange("p j t f -> p j (t f)"),
                                     w1_v[:, r, bass.ds(k * JB, JB), :]).then_inc(w1_in[par], 16)

                for f in range(FILLS):
                    load_tokens(0, f * FT, (f + 1) * FT, first_part_in[f])
                load_w1(0, 0)
                for t in range(1, DT):
                    load_tokens(t, 0, TT, part_in[t])
                with nc.allow_non_contiguous_dma(reason="b1 as columns"):
                    b1_v = a["L0_ffn_b1"].rearrange("(r g) s f -> r f (g s)", r=4)
                    for r in range(4):
                        sp.dma_start(b1[r * F:(r + 1) * F, :], b1_v[r]).then_inc(b1_in, 16)
                sp.dma_start(scratch["choices"], permT_all[:, :]).then_inc(choices_out, 16)

                def one(k, par):
                    if not first(k, 1):
                        sp.wait_ge(up_done, ev(k - 2, DT, DT - 1))
                    if not first(k):
                        load_w1(k, par)
                        store(k - 1, 1 - par)

                def store(k, par):
                    sp.wait_ge(hidden_made, ev(k, JB, JB - 1))
                    sp.dma_start(scratch["hidden"][bass.ds(k * JB, JB)].rearrange("j p n -> p j n"), hidden[par][:, :, :]).then_inc(hidden_out[par], 16)

                blocks(sp, one)
                store(BLKS - 1, 1)
                for n in range(2):
                    sp.wait_ge(hidden_out[n], 16 * (BLKS // 2))
                sp.wait_ge(choices_out, 16)

            @block.gpsimd
            def _(pool):
                make_masks(nc, pool, pieces, masks)
                pool.memset(ident[:, :], 0.0).then_inc(ident_made, 1)
                pool.wait_ge(ident_made, 1)
                pool.affine_select(out=ident[:, :], in_=ident[:, :], compare_op=ALU.not_equal, fill=1.0,
                                   base=0, pattern=[[-1, P]], channel_multiplier=1).then_inc(ident_made, 1)
                pool.wait_ge(masks, 3)

                def one(k, par):
                    for f in range(FILLS):
                        if first(k):
                            pool.wait_ge(perm_copied, min((f + 1) * FT, TT))
                        if not first(k, 1):
                            pool.wait_ge(gathered, ev(k - 2, PER, (DT - 1) * FILLS + f))
                        ts = slice(f * FT, (f + 1) * FT)
                        pool.tensor_tensor(pick[par][:, ts, :, :], perm[:, ts, bass.ds(k * EB, EB)].unsqueeze(3).broadcast_to([P, FT, EB, GP]),
                                           pieces[:, :].unsqueeze(1).unsqueeze(1).broadcast_to([P, FT, EB, GP]), ALU.mult).then_inc(pick_made, 1)

                blocks(pool, one)

            def evacuate(eng, which, k, parts):
                for t in parts:
                    for f in range(FILLS):
                        n = t * FILLS + f
                        if n % 2 != which:
                            continue
                        if f <= 1 and not (first(k) and t < 2):
                            eng.wait_ge(up_done, ev(k, DT, t - 2) if t >= 2 else ev(k - 1, DT, t + 2))
                        eng.wait_ge(gathered, ev(k, PER, n))
                        dst = chosen[t % 2][:, :, f * FT * GP:(f + 1) * FT * GP].rearrange("p e (t n) -> p t e n", n=GP)
                        src = ps[:, n % 4, 0:FT * EB * GP].rearrange("p (t e n) -> p t e n", t=FT, e=EB)
                        if which == 0:
                            eng.activation(dst, src, ACT.Copy, scale=1.0 / UP).then_inc(moved[0], 1)
                        else:
                            eng.tensor_scalar(dst, src, 1.0 / UP, None, ALU.mult).then_inc(moved[1], 1)

            @block.scalar
            def _(act):
                def one(k, par):
                    evacuate(act, 0, k, range(1))
                    if not first(k):
                        relu(k - 1, 1 - par)
                    evacuate(act, 0, k, range(1, DT))

                def relu(k, par):
                    act.wait_ge(up_done, ev(k, DT, DT - 1))
                    if first(k):
                        act.wait_ge(b1_in, 64)
                    if not first(k, 1):
                        act.wait_ge(hidden_out[par], 8 * (k - par))
                    for j in range(JB):
                        act.activation(hidden[par][:, j, :], ps[:, 4 + j, 0:N], ACT.Relu,
                                       bias=b1[:, bass.ds(k * JB + j, 1)]).then_inc(hidden_made, 1)

                blocks(act, one)
                relu(BLKS - 1, 1)

            @block.vector
            def _(dve):
                for t in range(TT):
                    dve.wait_ge(perm_turned, t + 1)
                    src = ps[:, 4 + t % 4, 0:P // 2].bitcast(F16).rearrange("p (r k j) -> p r k j", r=4, j=JB)
                    dst = perm[:, t, :].rearrange("p (k r j) -> p r k j", r=4, j=JB)
                    dve.tensor_copy(dst, src).then_inc(perm_copied, 1)

                def one(k, par):
                    evacuate(dve, 1, k, range(DT))

                blocks(dve, one)

            @block.tensor
            def _(pe):
                pe.wait_ge(ident_made, 2)
                for t in range(TT):
                    if t >= 4:
                        pe.wait_ge(perm_copied, t - 3)
                    pe.transpose(ps[:, 4 + t % 4, 0:P // 2].bitcast(F16), permT_all[:, t * P:(t + 1) * P], ident[:, :]).then_inc(perm_turned, 1)

                def gather(k, par, t):
                    if first(k) and t > 0:
                        pe.wait_ge(part_in[t], 16)
                    for f in range(FILLS):
                        n = t * FILLS + f
                        if first(k) and t == 0:
                            pe.wait_ge(first_part_in[f], 16)
                        if t == 0:
                            pe.wait_ge(pick_made, ev(k, FILLS, f))
                        if n >= 4:
                            pe.wait_ge(moved[n % 2], share_value(k, n - 4))
                        elif not first(k):
                            pe.wait_ge(moved[n % 2], share_value(k - 1, PER + n - 4))
                        for i in range(FT):
                            tt = f * FT + i
                            out = ps[:, n % 4, i * EB * GP:(i + 1) * EB * GP]
                            rhs = pick[par][:, tt, :, :].rearrange("p e n -> p (e n)")
                            for h in (1, 0):
                                mm = pe.matmul(out, tok[:, tt, t, h, :], rhs, start=(h == 1), stop=(h == 0))
                        mm.then_inc(gathered, 1)

                def share_value(k, n):
                    return ev(k, PER // 2, n // 2)

                def up(k, par, t):
                    n = (t + 1) * FILLS - 1
                    for m in (n, n - 1):
                        pe.wait_ge(moved[m % 2], share_value(k, m))
                    if t == 0:
                        pe.wait_ge(w1_in[par], 32 * (k - par) + 64)
                        if not first(k):
                            pe.wait_ge(hidden_made, ev(k - 1, JB, JB - 1))
                        else:
                            pe.wait_ge(perm_copied, TT)
                    for j in range(JB):
                        for r in range(4):
                            mm = pe.matmul(ps[r * F:(r + 1) * F, 4 + j, 0:N], w1[par][:, r, j, t, :], chosen[t % 2][:, r * JB + j, :],
                                           start=(t == 0), stop=(t == DT - 1))
                    mm.then_inc(up_done, 1)

                def one(k, par):
                    for t in range(DT):
                        gather(k, par, t)
                        if t > 0:
                            up(k, par, t - 1)
                        elif not first(k):
                            up(k - 1, 1 - par, DT - 1)

                blocks(pe, one)
                up(BLKS - 1, 1, DT - 1)


def experts_down(nc, sh, a, scratch, out):
    ES, F, N, DT, C, G = sh.ES, sh.F, sh.N, sh.DT, sh.C, sh.G
    NJ = ES // 4
    GB = 32
    NBLK = N // GB
    TB = GB * G
    JG = 4
    QW = C // 4
    HW = C // 2
    YT = QW // 32
    FQ = NJ // JG
    RING = 4
    TILES = TB // P
    PAIRS = TILES // 2
    w2_v = a["L0_ffn_W2"].rearrange("(r g) s (q y t) f -> r q y (g s) (t f)", r=4, q=4, t=YT)
    x2_v = scratch["x2"].rearrange("b q d -> (b q) d")
    out_v = out.rearrange("b q d -> (b q) d")
    hid_v = scratch["hidden"].rearrange("j p n -> p j n")

    with ExitStack() as es:
        def sb(name, shape, dt=F32):
            return es.enter_context(nc.sbuf_tensor(name, shape, dt))

        def sem(name):
            return es.enter_context(nc.semaphore(name))

        w2T = sb("w2T", [P, NJ, C])
        answers = sb("answers", [P, 2, GB, HW])
        w2_raw = answers[:, :, :, :].rearrange("p h n d -> p (h n d)").rearrange("p (q j t f) -> p q j t f", q=4, j=NJ, t=YT)
        stage = sb("stage", [P, 2, NJ, QW])
        hid = sb("hid", [P, NJ, GB])
        wide = sb("hidden_wide", [P, NJ, 4, GB])
        choices = sb("choices", [P, TB], F16)
        permR = sb("permR", [P, TB], F32R)
        b2H, b2L = (sb(f"b2{h}", [P, C], F32R) for h in "HL")
        x2 = sb("x2_pairs", [P, PAIRS, 2, HW])
        b2 = x2[:, PAIRS - 1, :, :].rearrange("p a d -> p (a d)")
        pieces = sb("pieces32", [P, 4])
        g_raw, gate = sb("g2_raw", [P, 1]), sb("gate2", [P, 1])
        ps = es.enter_context(nc.psum_tensor("ps_down", [P, 8, BANK], F32))

        w2_in = [sem(f"w2_in{n}") for n in range(8)]
        g_in, b2_in = sem("g_in"), sem("b2_in")
        masks, gate_done = sem("masks32_made"), sem("gate2_done")
        w2_turned = sem("w2_turned")
        b2_high, b2_low = sem("b2_high"), sem("b2_low")
        hid_in, choices_in = sem("hid_in"), sem("choices_in")
        wide_made = sem("wide_hidden_made")
        down, staged, turned = sem("down_done"), sem("staged"), sem("answers_turned")
        perm_cast = sem("perm_cast")
        summed, added = sem("summed"), sem("added")
        x2_in, x2_out = [sem(f"x2_in{n}") for n in range(PAIRS)], [sem(f"x2_out{n}") for n in range(PAIRS)]

        def known(k):
            return isinstance(k, int)

        def blocks(eng, one):
            one(0)
            one(1)
            with eng.Fori(2, NBLK - 1) as k:
                one(k)
            one(NBLK - 1)
            one(NBLK)

        def parts(k):
            return (k < NBLK, k >= 1) if known(k) else (True, True)

        def last(k):
            return known(k) and k == NBLK - 1

        def pair(k, h, i):
            return (2 * k + h) * PAIRS + i

        def sum_bank(i):
            return ps[:, RING + i, :].rearrange("p (a d) -> p a d", a=2)

        with nc.Block() as block:
            @block.sync
            def _(sp):
                def load_w2(q, half):
                    for r in range(4):
                        js = slice(half * NJ // 2, (half + 1) * NJ // 2)
                        sp.dma_start(w2_raw[r * 32:(r + 1) * 32, q, js, :, :].rearrange("y j t f -> y j (t f)"),
                                     w2_v[r, q, :, js, :]).then_inc(w2_in[2 * q + half], 16)

                def load_hidden(k):
                    sp.dma_start(hid[:, :, :], hid_v[:, :, bass.ds(k * GB, GB)]).then_inc(hid_in, 16)

                def load_choices(k):
                    sp.dma_start(choices[:, :], scratch["choices"][:, bass.ds(k * TB, TB)]).then_inc(choices_in, 16)

                def rows(v, k, h, i):
                    return v[bass.ds(k * TB + i * 2 * P, 2 * P), h * HW:(h + 1) * HW].rearrange("(a p) d -> p a d", a=2)

                def load_x2(k, h, i):
                    sp.dma_start(x2[:, i, :, :], rows(x2_v, k, h, i)).then_inc(x2_in[i], 16)

                load_w2(0, 0)
                load_hidden(0)
                load_w2(0, 1)
                load_choices(0)
                sp.dma_start(g_raw[:, :], a["g_ffn"].rearrange("(o c) -> o c", o=1).broadcast_to([P, 1])).then_inc(g_in, 16)
                sp.dma_start(b2, a["L0_ffn_b2"].rearrange("g s d -> (g s) d")).then_inc(b2_in, 16)
                for q in range(1, 4):
                    load_w2(q, 0)
                    load_w2(q, 1)
                for i in range(2):
                    load_x2(0, 0, i)

                def pairs(k, h):
                    for i in range(PAIRS):
                        sp.wait_ge(added, ev(pair(k, h, i), 1))
                        sp.dma_start(rows(out_v, k, h, i), x2[:, i, :, :]).then_inc(x2_out[i], 16)
                        i2, h2, k2 = (i + 2, h, k) if i + 2 < PAIRS else (i + 2 - PAIRS, 1 - h, k + h)
                        if known(k2) and k2 >= NBLK:
                            continue
                        if not (known(k) and k2 == 0 and h2 == 0):
                            sp.wait_ge(x2_out[i2], 16 * (2 * k2 + h2))
                        elif i2 == PAIRS - 1:
                            sp.wait_ge(b2_low, 1)
                        load_x2(k2, h2, i2)

                def one(k):
                    here, before = parts(k)
                    if before:
                        pairs(k - 1, 1)
                    if here and not (known(k) and k + 1 >= NBLK):
                        sp.wait_ge(wide_made, ev(k, FQ, FQ - 1))
                        load_hidden(k + 1)
                        sp.wait_ge(perm_cast, ev(k, 1))
                        load_choices(k + 1)
                    if here:
                        pairs(k, 0)

                blocks(sp, one)
                for b in range(PAIRS):
                    sp.wait_ge(x2_out[b], 16 * NBLK * 2)

            @block.gpsimd
            def _(pool):
                make_masks(nc, pool, pieces, masks)
                pool.wait_ge(masks, 3)

                def one(k):
                    if not parts(k)[0]:
                        return
                    pool.wait_ge(hid_in, 16 * ev(k, 1))
                    for g in range(FQ):
                        if not (known(k) and k == 0):
                            pool.wait_ge(down, ev(k - 1, 4 * FQ, 3 * FQ + g))
                        at = slice(g * JG, (g + 1) * JG)
                        pool.tensor_tensor(wide[:, at, :, :], hid[:, at, :].unsqueeze(2).broadcast_to([P, JG, 4, GB]),
                                           pieces[:, :].unsqueeze(1).unsqueeze(3).broadcast_to([P, JG, 4, GB]), ALU.mult).then_inc(wide_made, 1)

                blocks(pool, one)

            @block.scalar
            def _(act):
                act.wait_ge(g_in, 16)
                act.activation(gate[:, :], g_raw[:, :], ACT.Tanh).then_inc(gate_done, 1)
                act.wait_ge(b2_in, 16)
                act.activation(b2H[:, :], b2, ACT.Copy).then_inc(b2_high, 1)

                def one(k):
                    here, _ = parts(k)
                    if not here:
                        return
                    for q in range(4):
                        for g in range(FQ):
                            act.wait_ge(down, ev(k, 4 * FQ, q * FQ + g))
                            if g == 0 and not (known(k) and k == 0 and q < 2):
                                act.wait_ge(turned, ev(k, 4, q - 2) if q >= 2 else ev(k - 1, 4, q + 2))
                            act.activation(stage[:, q % 2, g * JG:(g + 1) * JG, :], ps[:, g % RING, :].rearrange("p (j d) -> p j d", j=JG),
                                           ACT.Copy).then_inc(staged, 1)
                        if q == 1:
                            act.wait_ge(choices_in, 16 * ev(k, 1))
                            if not (known(k) and k == 0):
                                act.wait_ge(summed, ev(pair(k - 1, 1, PAIRS - 1), 1))
                            act.activation(permR[:, :], choices[:, :], ACT.Copy).then_inc(perm_cast, 1)

                blocks(act, one)

            @block.vector
            def _(dve):
                def turn_w2(q):
                    for half in range(2):
                        js = slice(half * NJ // 2, (half + 1) * NJ // 2)
                        dve.wait_ge(w2_in[2 * q + half], 64)
                        dve.transpose(w2T[:, js, q * QW:(q + 1) * QW].rearrange("p j (y t) -> p j t y", t=YT),
                                      w2_raw[:, q, js, :, :]).then_inc(w2_turned, 1)

                turn_w2(0)
                dve.wait_ge(b2_high, 1)
                dve.tensor_tensor(b2L[:, :], b2, b2H[:, :].bitcast(F32), ALU.subtract).then_inc(b2_low, 1)
                turn_w2(1)
                turn_w2(2)
                dve.wait_ge(gate_done, 1)

                def turn(k, q):
                    dve.wait_ge(staged, ev(k, 4 * FQ, q * FQ + FQ - 1))
                    if known(k) and k == 0:
                        dve.wait_ge(w2_turned, 4 * (q // 2) + 4)
                    elif q % 2 == 0:
                        dve.wait_ge(summed, ev(pair(k - 1, q // 2, PAIRS - 1), 1))
                    at = slice(q % 2 * QW, q % 2 * QW + QW)
                    dve.transpose(answers[:, q // 2, :, at].rearrange("p n d -> p d n"),
                                  stage[:, q % 2, :, :].rearrange("p j d -> p d j")).then_inc(turned, 1)

                def add(k, h):
                    for i in range(PAIRS):
                        dve.wait_ge(summed, ev(pair(k, h, i), 1))
                        dve.wait_ge(x2_in[i], 16 * ev(2 * k + h, 1))
                        xt = x2[:, i, :, :]
                        dve.scalar_tensor_tensor(xt, sum_bank(i), gate[:, 0:1], xt, ALU.mult, ALU.add).then_inc(added, 1)

                def one(k):
                    here, before = parts(k)
                    if here:
                        turn(k, 0)
                    if before:
                        add(k - 1, 1)
                    if here:
                        turn(k, 1)
                        if known(k) and k == 0:
                            turn_w2(3)
                        turn(k, 2)
                        if last(k):
                            turn(k, 3)
                        add(k, 0)
                        if not last(k):
                            turn(k, 3)

                blocks(dve, one)

            @block.tensor
            def _(pe):
                def downs(k, q):
                    for g in range(FQ):
                        if known(k) and k == 0 and g % (FQ // 2) == 0:
                            pe.wait_ge(w2_turned, 2 * q + g // (FQ // 2) + 1)
                        if q == 0:
                            pe.wait_ge(wide_made, ev(k, FQ, g))
                        n = q * FQ + g
                        if n >= RING:
                            pe.wait_ge(staged, ev(k, 4 * FQ, n - RING))
                        elif not (known(k) and k == 0):
                            pe.wait_ge(staged, ev(k - 1, 4 * FQ, 4 * FQ + n - RING))
                        for i in range(JG):
                            j = g * JG + i
                            mm = pe.matmul(ps[:, g % RING, i * QW:(i + 1) * QW], wide[:, j, :, :].rearrange("p r n -> p (r n)"),
                                           w2T[:, j, q * QW:(q + 1) * QW], start=True, stop=True)
                        mm.then_inc(down, 1)

                def sums(k, h):
                    pe.wait_ge(turned, ev(k, 4, 2 * h + 1))
                    if h == 0:
                        pe.wait_ge(perm_cast, ev(k, 1))
                        if known(k) and k == 0:
                            pe.wait_ge(b2_low, 1)
                    at = slice(h * HW, (h + 1) * HW)
                    for i in range(PAIRS):
                        if not (known(k) and k == 0 and h == 0):
                            pe.wait_ge(added, ev(pair(k, h, i) - PAIRS, 1))
                        for o in range(2):
                            acc = sum_bank(i)[:, o, :]
                            t = 2 * i + o
                            who = permR[:, t * P:(t + 1) * P]
                            pe.matmul(acc, who, b2H[:, at], start=True, stop=False)
                            pe.matmul(acc, who, b2L[:, at], start=False, stop=False)
                            for g in range(P // G):
                                mm = pe.matmul(acc[g * G:(g + 1) * G, :], who[:, g * G:(g + 1) * G].bitcast(F32),
                                               answers[:, h, t * (P // G) + g, :], start=False, stop=True)
                        mm.then_inc(summed, 1)

                def one(k):
                    here, before = parts(k)
                    if here:
                        downs(k, 0)
                    if before:
                        sums(k - 1, 1)
                    if here:
                        downs(k, 1)
                        downs(k, 2)
                        if last(k):
                            downs(k, 3)
                        sums(k, 0)
                        if not last(k):
                            downs(k, 3)

                blocks(pe, one)


def flamingo_gated(nc, a, out):
    sh = Shapes(a["x"], a["ctx_1024"], a["L0_ffn_Wc"], a["L0_ffn_W1"])
    scratch = {
        "x2": nc.dram_tensor("x2_scratch", [sh.B, sh.Q, sh.C], F32, kind="Internal").ap(),
        "halves": nc.dram_tensor("halves_scratch", [sh.B, sh.Q, sh.DT, 2, P], F16, kind="Internal").ap(),
        "choices": nc.dram_tensor("choices_scratch", [P, sh.T], F16, kind="Internal").ap(),
        "hidden": nc.dram_tensor("hidden_scratch", [sh.ES // 4, P, sh.N], F32, kind="Internal").ap(),
    }
    with nc.sbuf_tensor("permT_all", [P, sh.T], F16) as permT_all:
        attention_and_routing(nc, sh, a, scratch, permT_all)
        experts_up(nc, sh, a, scratch, permT_all)
    experts_down(nc, sh, a, scratch, out)


_INS = ["x", "ctx_1024", "g_xattn", "g_ffn", "L0_xattn_Wq", "L0_xattn_bq", "L0_xattn_Wk", "L0_xattn_bk", "L0_xattn_Wv",
        "L0_xattn_bv", "L0_xattn_Wo", "L0_xattn_bo", "L0_ffn_Wc", "L0_ffn_bc", "L0_ffn_W1", "L0_ffn_b1", "L0_ffn_W2", "L0_ffn_b2"]


def kernel(**inputs):
    import numpy as _np
    import concourse.bacc as _bacc
    from concourse import mybir as _mybir
    from concourse.bass_utils import run_bass_kernel_spmd as _run

    nc = _bacc.Bacc("TRN2", target_bir_lowering=False, num_devices=1)
    arrays, aps = {}, {}
    for name in _INS:
        v = _np.ascontiguousarray(inputs[name])
        arrays[f"in_{name}"] = v
        aps[name] = nc.dram_tensor(f"in_{name}", v.shape, _mybir.dt.from_np(v.dtype), kind="ExternalInput").ap()
    out = nc.dram_tensor("out", inputs["x"].shape, _mybir.dt.float32, kind="ExternalOutput").ap()
    flamingo_gated(nc, aps, out)
    r = _run(nc, [arrays], core_ids=[0])
    return r.results[0]["out"]
```
